# Optimizing a Trainium2 kernel written in Bass

```python
import numpy as np
import jax
import jax.numpy as jnp

def _softmax(x, axis=-1):
    return jax.nn.softmax(x, axis=axis)

def _gelu(x):
    return jax.nn.gelu(x, approximate=True)

def _silu(x):
    return jax.nn.silu(x)

def _sigmoid(x):
    return jax.nn.sigmoid(x)

def _layernorm(x, axis=-1, eps=1e-05):
    m = jnp.mean(x, axis=axis, keepdims=True)
    v = jnp.var(x, axis=axis, keepdims=True)
    return (x - m) / jnp.sqrt(v + eps)

def _scatter_add(tgt, idx, src, axis=0):
    return tgt.at[idx].add(src)

def _segment_sum(src, seg, n):
    return jax.ops.segment_sum(src, seg, n)
kernel_name = 'mk_early_fusion_embed_d2_tok_img256_r4_e0e86b'

def setup_inputs(seed: int=0):
    np.random.seed(seed)
    _w = jnp.asarray

    def _rec_inputs():
        import jax
        import jax.numpy as jnp
        _rk = jax.random.key(seed)
        x = -0.000392918 + 0.999932 * jax.random.normal(jax.random.fold_in(_rk, 1), (4, 1, 128, 512), jnp.float32)
        x_txt = jax.random.randint(jax.random.fold_in(_rk, 51), (4, 128), 0, 127998, jnp.int32)
        return (x, x_txt)
    x, x_txt = _rec_inputs()

    def _L0_tok_setup():
        import jax, jax.numpy as jnp
        import numpy as np
        PATCH = 8
        EMBED = 64
        N_MELS = 128
        N_FRAMES = 512
        BATCH = 64
        NUM_PATCHES = N_MELS // PATCH * (N_FRAMES // PATCH)
        key = jax.random.key(seed)
        k1, k2, k3, k4 = jax.random.split(key, 4)
        x = jax.random.normal(k1, (BATCH, 1, N_MELS, N_FRAMES), dtype=jnp.float32)
        W = jax.random.normal(k2, (EMBED, PATCH * PATCH), dtype=jnp.float32) * (1.0 / np.sqrt(PATCH * PATCH))
        b = jax.random.normal(k3, (EMBED,), dtype=jnp.float32) * 0.01
        pos_embed = jax.random.normal(k4, (1, NUM_PATCHES, EMBED), dtype=jnp.float32) * 0.02
        return {'x': x, 'W': W, 'b': b, 'pos_embed': pos_embed}
    _L0_tok_all = _L0_tok_setup()
    _L0_tok_in = {k: v for k, v in _L0_tok_all.items() if k in ('W', 'b', 'pos_embed')}
    del _L0_tok_all

    def _L0_txt_setup():
        import jax, jax.numpy as jnp
        import numpy as np
        VOCAB = 32000
        HIDDEN = 512
        BATCH, SEQ = (4, 1024)
        key = jax.random.key(seed)
        k_ids, k_tab = jax.random.split(key)
        input_ids = jax.random.randint(k_ids, (BATCH, SEQ), 0, VOCAB, dtype=jnp.int32)
        ple_table = jax.random.normal(k_tab, (VOCAB, HIDDEN), dtype=jnp.float32)
        return {'input_ids': input_ids, 'ple_table': ple_table, 'layer_idx': 3, 'ple_dim': 64}
    _L0_txt_all = _L0_txt_setup()
    _L0_txt_in = {k: v for k, v in _L0_txt_all.items() if k in ('ple_table',)}
    del _L0_txt_all

    def _L0_attn_setup():
        import jax, jax.numpy as jnp
        import numpy as np
        B, N, D = (8, 512, 64)
        key = jax.random.key(seed)
        k1, k2, k3, k4 = jax.random.split(key, 4)
        s = D ** (-0.5)
        return {'x': jax.random.normal(k1, (B, N, D), dtype=jnp.float32), 'Wq': jax.random.normal(k2, (D, D), dtype=jnp.float32) * s, 'Wk': jax.random.normal(k3, (D, D), dtype=jnp.float32) * s, 'Wv': jax.random.normal(k4, (D, D), dtype=jnp.float32) * s}
    _L0_attn_all = _L0_attn_setup()
    _L0_attn_in = {k: v for k, v in _L0_attn_all.items() if k in ('Wq', 'Wk', 'Wv')}
    del _L0_attn_all

    def _L0_ffn_setup():
        import jax, jax.numpy as jnp
        import numpy as np
        DIM = 64
        HEADS = 8
        NUM_KEYS = 64
        NUM_KV = NUM_KEYS ** 2
        PK_TOPK = 16
        FINAL_TOPK = 16
        DIM_KEY = DIM // 2
        P = 2

        def _pk(x, Wq_pk, pk_keys):
            b, n, _ = x.shape
            q = (x @ Wq_pk).reshape(b, n, P, HEADS, DIM_KEY).transpose(2, 0, 1, 3, 4)
            sim = jnp.einsum('pbnhd,pkhd->pbnhk', q, pk_keys)
            scores, idx = jax.lax.top_k(sim, PK_TOPK)
            idx0 = idx[0]
            idx1 = idx[1] * NUM_KEYS
            index = (idx0[..., :, None] + idx1[..., None, :]).reshape(b, n, HEADS, PK_TOPK * PK_TOPK)
            score = (scores[0][..., :, None] + scores[1][..., None, :]).reshape(b, n, HEADS, PK_TOPK * PK_TOPK)
            final_scores, pk_idx = jax.lax.top_k(score, FINAL_TOPK)
            final_indices = jnp.take_along_axis(index, pk_idx, axis=-1)
            final_scores = jax.nn.softmax(final_scores, axis=-1)
            return (final_scores, final_indices)
        key = jax.random.key(seed)
        ks = jax.random.split(key, 7)
        b, n = (2, 256)
        std = 0.02
        x = jax.random.normal(ks[0], (b, n, DIM), dtype=jnp.float32)
        Wq_pk = jax.random.normal(ks[1], (DIM, P * HEADS * DIM_KEY), dtype=jnp.float32) * std
        pk_keys = jax.random.normal(ks[2], (P, NUM_KEYS, HEADS, DIM_KEY), dtype=jnp.float32) * std
        Wq = jax.random.normal(ks[3], (DIM, HEADS * DIM), dtype=jnp.float32) * std
        keys_table = jax.random.normal(ks[4], (NUM_KV * HEADS, DIM), dtype=jnp.float32) * std
        values_table = jax.random.normal(ks[5], (NUM_KV * HEADS, DIM), dtype=jnp.float32) * std
        Wo = jax.random.normal(ks[6], (DIM * HEADS, DIM), dtype=jnp.float32) * std
        return {'x': x, 'Wq_pk': Wq_pk, 'pk_keys': pk_keys, 'Wq': Wq, 'keys_table': keys_table, 'values_table': values_table, 'Wo': Wo}
    _L0_ffn_all = _L0_ffn_setup()
    _L0_ffn_in = {k: v for k, v in _L0_ffn_all.items() if k in ('Wq_pk', 'pk_keys', 'Wq', 'keys_table', 'values_table', 'Wo')}
    del _L0_ffn_all

    def _L1_attn_setup():
        import jax, jax.numpy as jnp
        import numpy as np
        D_MODEL = 64
        key = jax.random.key(seed)
        k_x, k_wqkv, k_bqkv, k_wp, k_bp = jax.random.split(key, 5)
        B, T, d = (4, 1024, D_MODEL)
        bound_qkv = 1.0 / np.sqrt(d)
        return {'x': jax.random.normal(k_x, (B, T, d), dtype=jnp.float32), 'W_qkv': jax.random.uniform(k_wqkv, (d, 3 * d), jnp.float32, -bound_qkv, bound_qkv), 'b_qkv': jax.random.uniform(k_bqkv, (3 * d,), jnp.float32, -bound_qkv, bound_qkv), 'W_proj': jax.random.uniform(k_wp, (d, d), jnp.float32, -bound_qkv, bound_qkv), 'b_proj': jax.random.uniform(k_bp, (d,), jnp.float32, -bound_qkv, bound_qkv)}
    _L1_attn_all = _L1_attn_setup()
    _L1_attn_in = {k: v for k, v in _L1_attn_all.items() if k in ('W_qkv', 'b_qkv', 'W_proj', 'b_proj')}
    del _L1_attn_all

    def _L1_ffn_setup():
        import jax, jax.numpy as jnp
        import numpy as np
        B, T, D, H, E = (16, 1024, 64, 128, 8)
        key = jax.random.key(seed)
        ks = jax.random.split(key, 5)
        x = jax.random.normal(ks[0], (B, T, D), dtype=jnp.float32)
        gate_w = jax.random.normal(ks[1], (D, E), dtype=jnp.float32) * 0.02
        gate_b = jnp.zeros((E,), dtype=jnp.float32)
        W1 = jax.random.normal(ks[2], (E, D, H), dtype=jnp.float32) * 0.02
        b1 = jnp.zeros((E, H), dtype=jnp.float32)
        W2 = jax.random.normal(ks[3], (E, H, D), dtype=jnp.float32) * 0.02
        b2 = jnp.zeros((E, D), dtype=jnp.float32)
        return {'x': x, 'gate_w': gate_w, 'gate_b': gate_b, 'W1': W1, 'b1': b1, 'W2': W2, 'b2': b2}
    _L1_ffn_all = _L1_ffn_setup()
    _L1_ffn_in = {k: v for k, v in _L1_ffn_all.items() if k in ('gate_w', 'gate_b', 'W1', 'b1', 'W2', 'b2')}
    del _L1_ffn_all
    return {'x': x, 'x_txt': x_txt, 'L0_tok_W': _L0_tok_in['W'], 'L0_tok_b': _L0_tok_in['b'], 'L0_tok_pos_embed': _L0_tok_in['pos_embed'], 'L0_txt_ple_table': _L0_txt_in['ple_table'], 'L0_attn_Wq': _L0_attn_in['Wq'], 'L0_attn_Wk': _L0_attn_in['Wk'], 'L0_attn_Wv': _L0_attn_in['Wv'], 'L0_ffn_Wq_pk': _L0_ffn_in['Wq_pk'], 'L0_ffn_pk_keys': _L0_ffn_in['pk_keys'], 'L0_ffn_Wq': _L0_ffn_in['Wq'], 'L0_ffn_keys_table': _L0_ffn_in['keys_table'], 'L0_ffn_values_table': _L0_ffn_in['values_table'], 'L0_ffn_Wo': _L0_ffn_in['Wo'], 'L1_attn_W_qkv': _L1_attn_in['W_qkv'], 'L1_attn_b_qkv': _L1_attn_in['b_qkv'], 'L1_attn_W_proj': _L1_attn_in['W_proj'], 'L1_attn_b_proj': _L1_attn_in['b_proj'], 'L1_ffn_gate_w': _L1_ffn_in['gate_w'], 'L1_ffn_gate_b': _L1_ffn_in['gate_b'], 'L1_ffn_W1': _L1_ffn_in['W1'], 'L1_ffn_b1': _L1_ffn_in['b1'], 'L1_ffn_W2': _L1_ffn_in['W2'], 'L1_ffn_b2': _L1_ffn_in['b2']}

def reference(x, x_txt, L0_tok_W, L0_tok_b, L0_tok_pos_embed, L0_txt_ple_table, L0_attn_Wq, L0_attn_Wk, L0_attn_Wv, L0_ffn_Wq_pk, L0_ffn_pk_keys, L0_ffn_Wq, L0_ffn_keys_table, L0_ffn_values_table, L0_ffn_Wo, L1_attn_W_qkv, L1_attn_b_qkv, L1_attn_W_proj, L1_attn_b_proj, L1_ffn_gate_w, L1_ffn_gate_b, L1_ffn_W1, L1_ffn_b1, L1_ffn_W2, L1_ffn_b2):
    import jax
    import jax.numpy as jnp

    def _L0_tok_ref(x, W, b, pos_embed):
        import jax, jax.numpy as jnp
        import numpy as np
        PATCH = 8
        EMBED = 64
        N_MELS = 128
        N_FRAMES = 512
        BATCH = 64
        NUM_PATCHES = N_MELS // PATCH * (N_FRAMES // PATCH)
        B = x.shape[0]
        mp, fp = (N_MELS // PATCH, N_FRAMES // PATCH)
        xs = x[:, 0]
        patches = xs.reshape(B, mp, PATCH, fp, PATCH).transpose(0, 1, 3, 2, 4).reshape(B, mp * fp, PATCH * PATCH)
        emb = jnp.einsum('bnk,ek->bne', patches, W) + b
        return emb + pos_embed

    def _L0_txt_ref(input_ids, ple_table, layer_idx, ple_dim):
        import jax, jax.numpy as jnp
        import numpy as np
        VOCAB = 32000
        HIDDEN = 512
        BATCH, SEQ = (4, 1024)
        start = layer_idx * ple_dim
        layer_slice = jax.lax.dynamic_slice_in_dim(ple_table, start, ple_dim, axis=1)
        return layer_slice[input_ids].astype(jnp.float32)

    def _L0_attn_ref(x, Wq, Wk, Wv):
        import jax, jax.numpy as jnp
        import numpy as np
        B, N, D = (8, 512, 64)
        q = jnp.einsum('bnd,ed->bne', x, Wq)
        k = jnp.einsum('bnd,ed->bne', x, Wk)
        v = jnp.einsum('bnd,ed->bne', x, Wv)
        energy = jnp.einsum('bqd,bkd->bqk', q, k)
        scaling = jnp.asarray(x.shape[-1] ** (-0.5), x.dtype)
        att = jax.nn.softmax(energy, axis=-1) * scaling
        out = jnp.einsum('bqk,bkv->bqv', att, v)
        return out

    def _L0_ffn_ref(x, Wq_pk, pk_keys, Wq, keys_table, values_table, Wo):
        import jax, jax.numpy as jnp
        import numpy as np
        DIM = 64
        HEADS = 8
        NUM_KEYS = 64
        NUM_KV = NUM_KEYS ** 2
        PK_TOPK = 16
        FINAL_TOPK = 16
        DIM_KEY = DIM // 2
        P = 2

        def _pk(x, Wq_pk, pk_keys):
            b, n, _ = x.shape
            q = (x @ Wq_pk).reshape(b, n, P, HEADS, DIM_KEY).transpose(2, 0, 1, 3, 4)
            sim = jnp.einsum('pbnhd,pkhd->pbnhk', q, pk_keys)
            scores, idx = jax.lax.top_k(sim, PK_TOPK)
            idx0 = idx[0]
            idx1 = idx[1] * NUM_KEYS
            index = (idx0[..., :, None] + idx1[..., None, :]).reshape(b, n, HEADS, PK_TOPK * PK_TOPK)
            score = (scores[0][..., :, None] + scores[1][..., None, :]).reshape(b, n, HEADS, PK_TOPK * PK_TOPK)
            final_scores, pk_idx = jax.lax.top_k(score, FINAL_TOPK)
            final_indices = jnp.take_along_axis(index, pk_idx, axis=-1)
            final_scores = jax.nn.softmax(final_scores, axis=-1)
            return (final_scores, final_indices)
        b, n, d = x.shape
        q = (x @ Wq).reshape(b, n, HEADS, DIM) * DIM ** (-0.5)
        kv_scores, indices = _pk(x, Wq_pk, pk_keys)
        offsets = jnp.arange(HEADS, dtype=indices.dtype) * NUM_KV
        ind = indices + offsets[None, None, :, None]
        k = jnp.einsum('bnhk,bnhkd->bnhd', kv_scores, keys_table[ind])
        v = jnp.einsum('bnhk,bnhkd->bnhd', kv_scores, values_table[ind])
        sim = jnp.einsum('bihd,bjhd->bhij', q, k)
        neg = -jnp.finfo(sim.dtype).max
        causal = jnp.tril(jnp.ones((n, n), dtype=bool))
        sim = jnp.where(causal, sim, neg)
        attn = jax.nn.softmax(sim, axis=-1)
        out = jnp.einsum('bhij,bjhd->bhid', attn, v)
        out = out.transpose(0, 2, 1, 3).reshape(b, n, HEADS * DIM)
        return out @ Wo

    def _L1_attn_ref(x, W_qkv, b_qkv, W_proj, b_proj):
        import jax, jax.numpy as jnp
        import numpy as np
        D_MODEL = 64
        B, T, d = x.shape
        qkv = x @ W_qkv + b_qkv
        q, k, v = jnp.split(qkv, 3, axis=-1)
        scale = 1.0 / np.sqrt(d).astype(np.float32)
        scores = jnp.einsum('btd,bsd->bts', q, k) * scale
        causal = jnp.tril(jnp.ones((T, T), dtype=bool))
        scores = jnp.where(causal, scores, -jnp.inf)
        weights = jax.nn.softmax(scores, axis=-1)
        ctx = jnp.einsum('bts,bsd->btd', weights, v)
        return ctx @ W_proj + b_proj

    def _L1_ffn_ref(x, gate_w, gate_b, W1, b1, W2, b2):
        import jax, jax.numpy as jnp
        import numpy as np
        B, T, D, H, E = (16, 1024, 64, 128, 8)
        Bb, Tt, Dd = x.shape
        Ee = gate_w.shape[1]
        xf = x.reshape(-1, Dd)
        N = xf.shape[0]
        logits = xf @ gate_w + gate_b
        probs = jax.nn.softmax(logits, axis=-1)
        top2_vals, top2_idx = jax.lax.top_k(probs, 2)
        cw = jnp.zeros((N, Ee), dtype=xf.dtype).at[jnp.arange(N)[:, None], top2_idx].add(top2_vals)

        def step(acc, params):
            w1, bb1, w2, bb2, we = params
            h = jax.nn.gelu(xf @ w1 + bb1, approximate=False)
            y = h @ w2 + bb2
            return (acc + we[:, None] * y, None)
        out, _ = jax.lax.scan(step, jnp.zeros_like(xf), (W1, b1, W2, b2, cw.T))
        return out.reshape(Bb, Tt, Dd)
    h = _L0_tok_ref(x, L0_tok_W, L0_tok_b, L0_tok_pos_embed)
    h = jnp.concatenate([h, _L0_txt_ref(x_txt, L0_txt_ple_table, 3, 64)], axis=1)
    h = h + _L0_attn_ref(_layernorm(h, axis=-1), L0_attn_Wq, L0_attn_Wk, L0_attn_Wv)
    h = h + _L0_ffn_ref(_layernorm(h, axis=-1), L0_ffn_Wq_pk, L0_ffn_pk_keys, L0_ffn_Wq, L0_ffn_keys_table, L0_ffn_values_table, L0_ffn_Wo)
    h = h + _L1_attn_ref(_layernorm(h, axis=-1), L1_attn_W_qkv, L1_attn_b_qkv, L1_attn_W_proj, L1_attn_b_proj)
    h = h + _L1_ffn_ref(_layernorm(h, axis=-1), L1_ffn_gate_w, L1_ffn_gate_b, L1_ffn_W1, L1_ffn_b1, L1_ffn_W2, L1_ffn_b2)
    return h

_drawn_inputs = setup_inputs


def setup_inputs(seed=0):
    import zlib

    import numpy as np

    out = dict(_drawn_inputs(seed))
    spreads = {'L1_ffn_gate_b': (0.0, 0.582), 'L1_ffn_b1': (0.0, 0.8), 'L1_ffn_b2': (0.0, 0.376)}
    factors = {'L0_tok_b': 5.633,
     'L0_tok_pos_embed': 2.864,
     'L0_ffn_Wq_pk': 8.0,
     'L0_ffn_pk_keys': 8.0,
     'L0_ffn_Wq': 64.0,
     'L0_ffn_keys_table': 55.291,
     'L0_ffn_values_table': 8.0,
     'L0_ffn_Wo': 8.0,
     'L1_ffn_gate_w': 2.869,
     'L1_ffn_W1': 8.0,
     'L1_ffn_W2': 8.0}
    for name, (base, spread) in spreads.items():
        noise = np.random.default_rng([zlib.crc32(name.encode()), seed]).standard_normal(out[name].shape)
        drawn = base * np.exp(spread * noise) if base else spread * noise
        out[name] = jnp.asarray(drawn.astype(out[name].dtype))
    for name, factor in factors.items():
        out[name] = (out[name] * factor).astype(out[name].dtype)
    return out
```

```python
from contextlib import ExitStack

import concourse.bass as bass
from concourse import mybir

F32 = mybir.dt.float32
BF16 = mybir.dt.bfloat16
I32 = mybir.dt.int32
U32 = mybir.dt.uint32
ALU = mybir.AluOpType
ACT = mybir.ActivationFunctionType
AX = mybir.AxisListType

P = 128
BATCH, MELS, FRAMES, PATCH = 4, 128, 512, 8
D = 64
PATCHES = (MELS // PATCH) * (FRAMES // PATCH)
TEXT = 128
TOKENS = PATCHES + TEXT
NT = TOKENS // P
PT_TILES = PATCHES // P
FJ = FRAMES // PATCH
VOCAB, PLE_GROUPS, PLE_LAYER = 32000, 8, 3
HEADS, KEYS, DK, TOPK = 8, 64, 32, 16
SLOTS = KEYS * KEYS
RING = 4
EXPERTS, HID = 8, 128
EPS = 1e-5
BANK = 512
LOWEST = -3.4028234663852886e38
MASKED = -1e30
PER_USE = 16 * TOPK
RSQRT_SEED = float(0x5F3759DF)
ROWS = [(a, TOPK // (a + 1)) for a in range(TOPK)]
CAND = sum(n for _, n in ROWS)
BLOCKS = []
_col = 0
for _a, _n in ROWS:
    if BLOCKS and BLOCKS[-1][2] == _n:
        BLOCKS[-1][1] += 1
    else:
        BLOCKS.append([_a, 1, _n, _col])
    _col += _n


def build(nc, x, ids, tok_wT, tok_b, pos, ple, wqT, wkT, wvT, wq_pk, keysT, wq_mem, kv_table, wo,
          w_qkv, b_qkv, w_proj, b_proj, gate_w, gate_b, w1, b1T, w2, b2, out):
    ctx = ExitStack()
    with ctx:
        def sb(name, shape, dt=F32):
            return ctx.enter_context(nc.sbuf_tensor(name, shape, dt))

        def ps(name, shape, dt=F32):
            return ctx.enter_context(nc.psum_tensor(name, shape, dt))

        def sem(name):
            return ctx.enter_context(nc.semaphore(name))

        ident = sb("ident", [P, P])
        ident_h = sb("ident_h", [P, P], BF16)
        causal = sb("causal", [P, P], BF16)
        iota_c = sb("iota_c", [P, CAND])
        head_off = sb("head_off", [P, HEADS])
        tokw = sb("tokw", [D, D])
        posb = sb("posb", [P, PT_TILES, D])
        tokb = sb("tokb", [P, D])
        w0 = sb("w0", [D, 3, D])
        wpk = sb("wpk", [D, 2 * HEADS * DK])
        keys_bd = sb("keys_bd", [P, 4, 4 * KEYS])
        wqm = sb("wqm", [D, HEADS * D])
        wo_s = sb("wo_s", [P, 4, D])
        wqkv = sb("wqkv", [D, 3 * D])
        bq = sb("bq", [D, 2])
        bq8 = sb("bq8", [D, 1])
        bv = sb("bv", [P, D])
        wproj = sb("wproj", [D, D])
        bproj = sb("bproj", [P, D])
        gw = sb("gw", [D, EXPERTS])
        gb = sb("gb", [P, EXPERTS])
        w1_s = sb("w1_s", [D, EXPERTS, HID])
        b1_s = sb("b1_s", [HID, EXPERTS])
        w2_s = sb("w2_s", [HID, EXPERTS, D])
        b2_s = sb("b2_s", [P, EXPERTS, D])
        ids_s = sb("ids_s", [P, BATCH], I32)
        ids_f = sb("ids_f", [P, 2, BATCH])
        ids_u = sb("ids_u", [P, BATCH], U32)
        text = sb("text", [P, BATCH, D])

        h = sb("h", [P, BATCH * NT, D])
        patch = sb("patch", [P, PT_TILES, D])
        patchT = sb("patchT", [D, P])
        st6 = sb("st6", [P, 6])
        mv = sb("mv", [P, 2])
        rs = sb("rs", [P, 8])
        rsi = sb("rsi", [P, 2], I32)
        xn = sb("xn", [P, D])
        xnT = sb("xnT", [D, P])
        qk0 = sb("qk0", [D, 2, TOKENS])
        v0 = sb("v0", [P, NT, D])
        xn2T = sb("xn2T", [D, NT, P])
        probs = sb("probs", [P, TOKENS])
        probsT = sb("probsT", [P, TOKENS])
        nmax = sb("nmax", [P, 1])
        rsum = sb("rsum", [P, 2])
        rinv = sb("rinv", [P, 2])
        qpkT = sb("qpkT", [P, BANK])
        sims = sb("sims", [P, 2 * HEADS, KEYS])
        sims2 = sb("sims2", [P, 2 * HEADS, KEYS])
        top_v = sb("top_v", [P, 2 * HEADS, TOPK])
        top_i = sb("top_i", [P, 2 * HEADS, TOPK], U32)
        top_f = sb("top_f", [P, 2 * HEADS, TOPK])
        cand_v = sb("cand_v", [P, HEADS, CAND])
        cand_v2 = sb("cand_v2", [P, HEADS, CAND])
        cand_i = sb("cand_i", [P, HEADS, CAND])
        fin_v = sb("fin_v", [P, HEADS, TOPK])
        fin_p = sb("fin_p", [P, HEADS, TOPK], U32)
        fin_f = sb("fin_f", [P, HEADS, TOPK])
        hot = sb("hot", [P, 2 * TOPK, CAND])
        row_f = sb("row_f", [P, HEADS * TOPK])
        w_sum = sb("w_sum", [P, 2, HEADS])
        row_i = sb("row_i", [P, NT, HEADS * TOPK], U32)
        row_w = sb("row_w", [P, NT, HEADS, TOPK])
        rows = sb("rows", [P, RING, TOPK, 2 * D])
        kv = sb("kv", [P, NT, 2, HEADS, D])
        kT = sb("kT", [P, 4, TOKENS])
        qmT = sb("qmT", [P, BANK])
        cx = sb("cx", [P, BANK])
        cxT = sb("cxT", [P, BANK])
        q1T = sb("q1T", [D, P])
        k1T = sb("k1T", [D, TOKENS])
        v1 = sb("v1", [P, NT, D])
        gate = sb("gate", [P, 8, EXPERTS])
        gelT = sb("gelT", [HID, EXPERTS, P])
        ysc = sb("ysc", [P, EXPERTS, D])
        ysum = sb("ysum", [P, D])
        outt = sb("outt", [P, D])

        pS = ps("pS", [P, 3 * BANK])
        pT = ps("pT", [P, 3 * BANK])
        pM = ps("pM", [P, BANK])
        pO = ps("pO", [P, BANK])

        const_loaded = sem("const_loaded")
        w_loaded_pe = sem("w_loaded_pe")
        w_loaded_act = sem("w_loaded_act")
        w_loaded_dve = sem("w_loaded_dve")
        keys_zeroed = sem("keys_zeroed")
        keys_loaded = sem("keys_loaded")
        ids_loaded = sem("ids_loaded")
        pool_step = sem("pool_step")
        masks_ready = sem("masks_ready")
        masks_ready_dve = sem("masks_ready_dve")
        text_ids_ready = sem("text_ids_ready")
        text_loaded = sem("text_loaded")
        bq8_ready = sem("bq8_ready")
        patch_loaded = sem("patch_loaded")
        patch_free = sem("patch_free")
        dve_step = sem("dve_step")
        patchT_ready = sem("patchT_ready")
        patchT_copied = sem("patchT_copied")
        emb_ready = sem("emb_ready")
        xn_ready = sem("xn_ready")
        xn_free = sem("xn_free")
        xnT_ready = sem("xnT_ready")
        xnT_copied = sem("xnT_copied")
        qkv0_ready = sem("qkv0_ready")
        qkv0_copied = sem("qkv0_copied")
        scores_ready = sem("scores_ready")
        negmax_ready = sem("negmax_ready")
        probs_ready = sem("probs_ready")
        probsT_ready = sem("probsT_ready")
        probsT_copied = sem("probsT_copied")
        ctx_ready = sem("ctx_ready")
        qpk_ready = sem("qpk_ready")
        qpk_copied = sem("qpk_copied")
        sims_ready = sem("sims_ready")
        sims_copied = sem("sims_copied")
        sims_seen = sem("sims_seen")
        fin_ready = sem("fin_ready")
        fin_exp = sem("fin_exp")
        rows_chosen = sem("rows_chosen")
        rows_landed = [sem(f"rows_landed{n}") for n in range(RING)]
        rows_seen = sem("rows_seen")
        slot_free = [sem(f"slot_free{n}") for n in range(RING)]
        kv_ready = sem("kv_ready")
        kq_ready = sem("kq_ready")
        kq_copied = sem("kq_copied")
        heads_ready = sem("heads_ready")
        headsT_ready = sem("headsT_ready")
        headsT_copied = sem("headsT_copied")
        mem_out_ready = sem("mem_out_ready")
        qkv1_ready = sem("qkv1_ready")
        qkv1_ready_dve = sem("qkv1_ready_dve")
        qk1_copied = sem("qk1_copied")
        v1_ready = sem("v1_ready")
        logits_ready = sem("logits_ready")
        logits_shifted = sem("logits_shifted")
        gate_exp = sem("gate_exp")
        hidden_ready = sem("hidden_ready")
        gelu_ready = sem("gelu_ready")
        experts_ready = sem("experts_ready")
        out_ready = sem("out_ready")
        out_stored = sem("out_stored")

        block = ctx.enter_context(nc.Block())

        @block.sync
        def _(sp):
            sp.dma_start(ids_s[:], ids).then_inc(ids_loaded, 16)

            def load_patches(b):
                for m in range(MELS // PATCH):
                    src = x[b, 0, m * PATCH:(m + 1) * PATCH, :].rearrange("p (j f) -> j p f", f=PATCH)
                    dst = patch[FJ * (m % 2):FJ * (m % 2) + FJ, m // 2, :].rearrange("j (p f) -> j p f", f=PATCH)
                    sp.dma_start(dst, src).then_inc(patch_loaded, 16)

            load_patches(0)
            loads = [
                (tokw[:], tok_wT), (posb[:], pos.rearrange("(t p) e -> p t e", p=P)),
                (tokb[:], tok_b.partition_broadcast(P)),
                (w0[:, 0, :], wqT), (w0[:, 1, :], wkT), (w0[:, 2, :], wvT),
                (wpk[:], wq_pk), (wqm[:], wq_mem), (wo_s[:], wo.rearrange("(c p) e -> p c e", p=P)),
                (wqkv[:], w_qkv), (bq[:, 0:1], b_qkv[0:D].unsqueeze(1)), (bq[:, 1:2], b_qkv[D:2 * D].unsqueeze(1)),
                (bv[:], b_qkv[2 * D:3 * D].partition_broadcast(P)),
                (wproj[:], w_proj), (bproj[:], b_proj.partition_broadcast(P)),
                (gw[:], gate_w), (gb[:], gate_b.partition_broadcast(P)),
                (w1_s[:], w1.rearrange("e d k -> d e k")),
                (b1_s[:], b1T), (w2_s[:], w2.rearrange("e k d -> k e d")),
                (b2_s[:].rearrange("p e d -> p (e d)"), b2.rearrange("e d -> (e d)").partition_broadcast(P)),
            ]
            for dst, src in loads:
                sp.dma_start(dst, src).then_inc(const_loaded, 16)
            sp.wait_ge(const_loaded, 16 * len(loads))
            for s in (w_loaded_pe, w_loaded_act, w_loaded_dve):
                sp.sem_inc(s, 1)
            sp.wait_ge(keys_zeroed, 1)
            for p in range(2):
                for g in range(HEADS):
                    r = DK * (g % 4)
                    sp.dma_start(keys_bd[r:r + DK, 2 * p + g // 4, KEYS * (g % 4):KEYS * (g % 4) + KEYS],
                                 keysT[p, g]).then_inc(keys_loaded, 16)
            for b in range(1, BATCH):
                sp.wait_ge(patch_free, 1)
                sp.sem_inc(patch_free, -1)
                load_patches(b)

        @block.gpsimd
        def _(pool):
            def step(ins):
                ins.then_inc(pool_step, 1)
                pool.wait_ge(pool_step, 1)
                pool.sem_inc(pool_step, -1)

            pool.memset(keys_bd[:], 0.0).then_inc(keys_zeroed, 1)
            step(pool.memset(ident[:], 0.0))
            step(pool.affine_select(out=ident[:], in_=ident[:], compare_op=ALU.not_equal, fill=1.0, base=0,
                                    pattern=[[-1, P]], channel_multiplier=1))
            step(pool.tensor_copy(ident_h[:], ident[:]))
            step(pool.memset(causal[:], 0.0))
            step(pool.affine_select(out=causal[:], in_=causal[:], compare_op=ALU.is_ge, fill=MASKED, base=0,
                                    pattern=[[-1, P]], channel_multiplier=1))
            step(pool.iota(iota_c[:], pattern=[[1, CAND]], base=0, channel_multiplier=0,
                           allow_small_or_imprecise_dtypes=True))
            step(pool.iota(head_off[:], pattern=[[SLOTS, HEADS]], base=0, channel_multiplier=0,
                           allow_small_or_imprecise_dtypes=True))
            pool.sem_inc(masks_ready, 1)
            pool.sem_inc(masks_ready_dve, 1)
            pool.wait_ge(text_ids_ready, 1)
            pool.sem_inc(text_ids_ready, -1)
            for b in range(BATCH):
                pool.indirect_dma_start(
                    out=text[:, b, :], out_offset=None, in_=ple,
                    in_offset=bass.IndirectOffsetOnAxis(ap=ids_u[:, b:b + 1], axis=0)).then_inc(text_loaded, 16)

            with pool.Fori(0, BATCH) as _b:
                for i in range(NT):
                    pool.wait_ge(rows_chosen, 1)
                    pool.sem_inc(rows_chosen, -1)
                    for g in range(HEADS):
                        pool.wait_ge(slot_free[g % RING], 1)
                        pool.sem_inc(slot_free[g % RING], -1)
                        for r in range(TOPK):
                            c = g * TOPK + r
                            pool.indirect_dma_start(
                                out=rows[:, g % RING, r, :], out_offset=None, in_=kv_table,
                                in_offset=bass.IndirectOffsetOnAxis(ap=row_i[:, i, c:c + 1], axis=0),
                            ).then_inc(rows_landed[g % RING], 16)

        @block.tensor
        def _(pe):
            mm = nc.tensor.matmul

            def transpose_xn():
                pe.wait_ge(xn_ready, 1)
                pe.sem_inc(xn_ready, -1)
                nc.tensor.transpose(pM[0:D, 0:P], xn[:], ident[:]).then_inc(xnT_ready, 1)
                pe.wait_ge(xnT_copied, 1)
                pe.sem_inc(xnT_copied, -1)
                pe.sem_inc(xn_free, 1)

            def attend(heads):
                def scores(q, k, _v, n, masked):
                    for c in range(0, n * P, BANK):
                        e = min(c + BANK, n * P)
                        diag = masked and e == n * P
                        last = mm(pS[:, c:e], q, k[:, c:e], start=True, stop=not diag)
                        if diag:
                            last = mm(pS[:, e - P:e], ident_h[:], causal[:], start=False, stop=True)
                    last.then_inc(scores_ready, 1)

                scores(*heads[0])
                for m, (_q, _k, v, n, _) in enumerate(heads):
                    pe.wait_ge(probs_ready, 1)
                    pe.sem_inc(probs_ready, -1)
                    for j in range(n):
                        last = nc.tensor.transpose(pT[:, j * P:(j + 1) * P], probs[:, j * P:(j + 1) * P], ident[:])
                    last.then_inc(probsT_ready, 1)
                    if m + 1 < len(heads):
                        scores(*heads[m + 1])
                    pe.wait_ge(probsT_copied, 1)
                    pe.sem_inc(probsT_copied, -1)
                    for j in range(n):
                        last = mm((pO, pM)[m % 2][:, 0:D], probsT[:, j * P:(j + 1) * P], v(j),
                                  start=(j == 0), stop=(j == n - 1))
                    last.then_inc(ctx_ready, 1)

            def front():
                for i in range(NT):
                    if i < PT_TILES:
                        if i == 0:
                            pe.wait_ge(patch_loaded, 16 * (MELS // PATCH))
                            pe.sem_inc(patch_loaded, -(16 * (MELS // PATCH)))
                        nc.tensor.transpose(pM[0:D, 0:P], patch[:, i, :], ident[:]).then_inc(patchT_ready, 1)
                        pe.wait_ge(patchT_copied, 1)
                        pe.sem_inc(patchT_copied, -1)
                        mm(pO[:, 0:D], patchT[:], tokw[:], start=True, stop=True).then_inc(emb_ready, 1)
                    transpose_xn()
                    mm(pM[0:D, 0:P], w0[:, 0, :], xnT[:], start=True, stop=True)
                    mm(pM[0:D, P:2 * P], w0[:, 1, :], xnT[:], start=True, stop=True)
                    mm(pM[:, 2 * P:2 * P + D], xnT[:], w0[:, 2, :], start=True, stop=True).then_inc(qkv0_ready, 1)
                    pe.wait_ge(qkv0_copied, 1)
                    pe.sem_inc(qkv0_copied, -1)
                pe.sem_inc(patch_free, 1)

            def select(i):
                attend([(qk0[:, 0, i * P:(i + 1) * P], qk0[:, 1, :], lambda j: v0[:, j, :], NT, False)])
                transpose_xn()
                for c in range(4):
                    last = mm(pM[:, c * P:(c + 1) * P], wpk[:, c * P:(c + 1) * P], xn2T[:, i, :], start=True, stop=True)
                last.then_inc(qpk_ready, 1)
                pe.wait_ge(qpk_copied, 1)
                pe.sem_inc(qpk_copied, -1)
                for c in range(4):
                    last = mm(pS[:, c * 256:(c + 1) * 256], qpkT[:, c * P:(c + 1) * P], keys_bd[:, c, :],
                              start=True, stop=True)
                last.then_inc(sims_ready, 1)
                pe.wait_ge(sims_seen, 1)
                pe.sem_inc(sims_seen, -1)

            def back(i):
                pe.wait_ge(kv_ready, 1)
                pe.sem_inc(kv_ready, -1)
                for c in range(4):
                    nc.tensor.transpose(pT[:, c * P:(c + 1) * P], kv[:, i, 0, 2 * c:2 * c + 2, :].rearrange("p g d -> p (g d)"), ident[:])
                for c in range(4):
                    last = mm(pM[:, c * P:(c + 1) * P], wqm[:, c * P:(c + 1) * P], xn2T[:, i, :], start=True, stop=True)
                last.then_inc(kq_ready, 1)
                pe.wait_ge(kq_copied, 1)
                pe.sem_inc(kq_copied, -1)
                heads = []
                for g in range(HEADS):
                    r = D * (g % 2)
                    heads.append((qmT[r:r + D, (g // 2) * P:(g // 2 + 1) * P], kT[r:r + D, g // 2, :],
                                  lambda j, g=g: kv[:, j, 1, g, :], i + 1, True))
                attend(heads)
                pe.wait_ge(heads_ready, 1)
                pe.sem_inc(heads_ready, -1)
                for c in range(4):
                    last = nc.tensor.transpose(pM[:, c * P:(c + 1) * P], cx[:, c * P:(c + 1) * P], ident[:])
                last.then_inc(headsT_ready, 1)
                pe.wait_ge(headsT_copied, 1)
                pe.sem_inc(headsT_copied, -1)
                for c in range(4):
                    last = mm(pO[:, 0:D], cxT[:, c * P:(c + 1) * P], wo_s[:, c, :], start=(c == 0), stop=(c == 3))
                last.then_inc(mem_out_ready, 1)
                transpose_xn()
                mm(pM[0:D, 0:P], wqkv[:, 0:D], xnT[:], start=True, stop=True)
                mm(pM[0:D, P:2 * P], wqkv[:, D:2 * D], xnT[:], start=True, stop=True).then_inc(qkv1_ready, 1)
                mm(pO[:, 0:D], xnT[:], wqkv[:, 2 * D:3 * D], start=True, stop=True)\
                    .then_inc(qkv1_ready_dve, 1)
                pe.wait_ge(qk1_copied, 1)
                pe.sem_inc(qk1_copied, -1)
                pe.wait_ge(v1_ready, 1)
                pe.sem_inc(v1_ready, -1)
                attend([(q1T[:], k1T[:], lambda j: v1[:, j, :], i + 1, True)])
                pe.wait_ge(heads_ready, 1)
                pe.sem_inc(heads_ready, -1)
                nc.tensor.transpose(pM[0:D, 0:P], cx[:, 0:D], ident[:]).then_inc(headsT_ready, 1)
                pe.wait_ge(headsT_copied, 1)
                pe.sem_inc(headsT_copied, -1)
                mm(pO[:, 0:D], cxT[0:D, 0:P], wproj[:], start=True, stop=True).then_inc(mem_out_ready, 1)
                transpose_xn()
                mm(pM[:, 0:EXPERTS], xnT[:], gw[:], start=True, stop=True).then_inc(logits_ready, 1)
                for e in range(EXPERTS):
                    last = mm(pS[:, e * P:(e + 1) * P], w1_s[:, e, :], xnT[:], start=True, stop=True)
                last.then_inc(hidden_ready, 1)
                pe.wait_ge(gelu_ready, 1)
                pe.sem_inc(gelu_ready, -1)
                for e in range(EXPERTS):
                    last = mm(pO[:, e * D:(e + 1) * D], gelT[:, e, :], w2_s[:, e, :], start=True, stop=True)
                last.then_inc(experts_ready, 1)

            pe.wait_ge(masks_ready, 1)
            pe.sem_inc(masks_ready, -1)
            pe.wait_ge(w_loaded_pe, 1)
            pe.sem_inc(w_loaded_pe, -1)
            front()
            pe.wait_ge(keys_loaded, 16 * 2 * HEADS)
            for i in range(NT):
                select(i)
            with pe.Fori(0, BATCH - 1):
                front()
                for i in range(NT):
                    back(i)
                    select(i)
            for i in range(NT):
                back(i)

        @block.scalar
        def _(act):
            def copy(dst, src, done, scale=1.0):
                nc.scalar.activation(dst, src, ACT.Copy, scale=scale).then_inc(done, 1)

            def copy_xnT(dst):
                act.wait_ge(xnT_ready, 1)
                act.sem_inc(xnT_ready, -1)
                copy(dst, pM[0:D, 0:P], xnT_copied)

            def attend(lengths):
                for m, n in enumerate(lengths):
                    act.wait_ge(negmax_ready, 1)
                    act.sem_inc(negmax_ready, -1)
                    nc.scalar.activation(probs[:, 0:n * P], pS[:, 0:n * P], ACT.Exp, bias=nmax[:],
                                         accum_out=rsum[:, m % 2:m % 2 + 1]).then_inc(probs_ready, 1)
                    act.wait_ge(probsT_ready, 1)
                    act.sem_inc(probsT_ready, -1)
                    copy(probsT[:, 0:n * P], pT[:, 0:n * P], probsT_copied)

            def front():
                for i in range(NT):
                    if i < PT_TILES:
                        act.wait_ge(patchT_ready, 1)
                        act.sem_inc(patchT_ready, -1)
                        copy(patchT[:], pM[0:D, 0:P], patchT_copied)
                    copy_xnT(xnT[:])
                    act.wait_ge(qkv0_ready, 1)
                    act.sem_inc(qkv0_ready, -1)
                    nc.scalar.activation(qk0[:, :, i * P:(i + 1) * P],
                                         pM[0:D, 0:2 * P].rearrange("d (w t) -> d w t", w=2), ACT.Copy)
                    copy(v0[:, i, :], pM[:, 2 * P:2 * P + D], qkv0_copied)

            def select(i):
                attend([NT])
                copy_xnT(xn2T[:, i, :])
                act.wait_ge(qpk_ready, 1)
                act.sem_inc(qpk_ready, -1)
                copy(qpkT[:], pM[:], qpk_copied)
                act.wait_ge(sims_ready, 1)
                act.sem_inc(sims_ready, -1)
                copy(sims[:].rearrange("p g k -> p (g k)"), pS[:, 0:2 * HEADS * KEYS], sims_copied)
                act.wait_ge(fin_ready, 1)
                act.sem_inc(fin_ready, -1)
                nc.scalar.activation(row_w[:, i, :, :], fin_v[:], ACT.Exp).then_inc(fin_exp, 1)

            def store(b, i):
                act.wait_ge(out_ready, 1)
                act.sem_inc(out_ready, -1)
                act.dma_start(out[b, i * P:(i + 1) * P, :], outt[:]).then_inc(out_stored, 16)

            def back(b, i):
                act.wait_ge(kq_ready, 1)
                act.sem_inc(kq_ready, -1)
                nc.scalar.activation(kT[:, :, i * P:(i + 1) * P],
                                     pT[:, 0:4 * P].rearrange("p (c t) -> p c t", c=4), ACT.Copy)
                copy(qmT[:], pM[:], kq_copied, scale=D ** -0.5)
                attend([i + 1] * HEADS)
                act.wait_ge(headsT_ready, 1)
                act.sem_inc(headsT_ready, -1)
                copy(cxT[:], pM[:], headsT_copied)
                copy_xnT(xnT[:])
                act.wait_ge(qkv1_ready, 1)
                act.sem_inc(qkv1_ready, -1)
                nc.scalar.activation(q1T[:], pM[0:D, 0:P], ACT.Identity, bias=bq8[:], scale=D ** -0.5)
                nc.scalar.activation(k1T[:, i * P:(i + 1) * P], pM[0:D, P:2 * P], ACT.Identity,
                                     bias=bq[:, 1:2]).then_inc(qk1_copied, 1)
                attend([i + 1])
                act.wait_ge(headsT_ready, 1)
                act.sem_inc(headsT_ready, -1)
                copy(cxT[0:D, 0:P], pM[0:D, 0:P], headsT_copied)
                copy_xnT(xnT[:])
                act.wait_ge(logits_shifted, 1)
                act.sem_inc(logits_shifted, -1)
                nc.scalar.activation(gate[:, 1, :], gate[:, 0, :], ACT.Exp,
                                     accum_out=w_sum[:, 1, 0:1]).then_inc(gate_exp, 1)
                act.wait_ge(hidden_ready, 1)
                act.sem_inc(hidden_ready, -1)
                for e in range(EXPERTS):
                    last = nc.scalar.activation(gelT[:, e, :], pS[:, e * P:(e + 1) * P], ACT.Gelu,
                                                bias=b1_s[:, e:e + 1])
                last.then_inc(gelu_ready, 1)
                store(b, i)

            act.wait_ge(w_loaded_act, 1)
            act.sem_inc(w_loaded_act, -1)
            nc.scalar.activation(bq8[:], bq[:, 0:1], ACT.Copy, scale=D ** -0.5).then_inc(bq8_ready, 1)
            act.wait_ge(bq8_ready, 1)
            act.sem_inc(bq8_ready, -1)
            front()
            for i in range(NT):
                select(i)
            with act.Fori(0, BATCH - 1) as b:
                front()
                for i in range(NT):
                    back(b, i)
                    select(i)
            for i in range(NT):
                back(BATCH - 1, i)
            act.wait_ge(out_stored, 16)

        @block.vector
        def _(dve):
            V = nc.vector

            def step(ins):
                ins.then_inc(dve_step, 1)
                dve.wait_ge(dve_step, 1)
                dve.sem_inc(dve_step, -1)

            def layer_norm(src):
                step(V.bn_stats(st6[:], src))
                step(V.bn_aggr(mv[:], st6[:]))
                step(V.tensor_scalar(rs[:, 0:1], mv[:, 1:2], EPS, None, ALU.add))
                V.tensor_scalar(rs[:, 1:2], rs[:, 0:1], 0.5, None, ALU.mult)
                step(V.tensor_scalar(rsi[:, 0:1], rs[:, 0:1].bitcast(I32), 1, None, ALU.logical_shift_right))
                step(V.tensor_scalar(rs[:, 2:3].bitcast(I32), rsi[:, 0:1], -1.0, RSQRT_SEED, ALU.mult, ALU.add))
                y = 2
                for _ in range(3):
                    step(V.scalar_tensor_tensor(rs[:, 4:5], rs[:, y:y + 1], rs[:, 1:2], rs[:, y:y + 1],
                                                ALU.mult, ALU.mult))
                    step(V.scalar_tensor_tensor(rs[:, 5 - y:6 - y], rs[:, 4:5], 1.5, rs[:, y:y + 1],
                                                ALU.subtract, ALU.mult, reverse0=True))
                    y = 5 - y
                dve.wait_ge(xn_free, 1)
                dve.sem_inc(xn_free, -1)
                V.tensor_scalar(xn[:], src, mv[:, 0:1], rs[:, y:y + 1], ALU.subtract, ALU.mult).then_inc(xn_ready, 1)

            def row_max(n):
                dve.wait_ge(scores_ready, 1)
                dve.sem_inc(scores_ready, -1)
                V.tensor_reduce(nmax[:], pS[:, 0:n * P], AX.X, ALU.max, negate=True).then_inc(negmax_ready, 1)

            def attend(lengths, finish):
                row_max(lengths[0])
                for m in range(len(lengths)):
                    if m + 1 < len(lengths):
                        row_max(lengths[m + 1])
                    dve.wait_ge(ctx_ready, 1)
                    dve.sem_inc(ctx_ready, -1)
                    o = m % 2
                    step(V.reciprocal(rinv[:, o:o + 1], rsum[:, o:o + 1]))
                    finish(m, (pO, pM)[o][:, 0:D], rinv[:, o:o + 1])

            def front(b):
                for i in range(NT):
                    hs = h[:, b * NT + i, :]
                    if i < PT_TILES:
                        dve.wait_ge(emb_ready, 1)
                        dve.sem_inc(emb_ready, -1)
                        step(V.tensor_tensor(hs, pO[:, 0:D], posb[:, i, :], ALU.add))
                    else:
                        step(V.tensor_copy(hs, text[:, b, :]))
                    layer_norm(hs)

            def top16(values, spare, best, where, groups):
                for g in range(groups):
                    last = V.max(best[:, g, 0:8], values[:, g, :])
                step(last)
                for g in range(groups):
                    V.max_index(where[:, g, 0:8], best[:, g, 0:8], values[:, g, :])
                    last = V.match_replace(spare[:, g, :], best[:, g, 0:8], values[:, g, :], LOWEST)
                step(last)
                for g in range(groups):
                    last = V.max(best[:, g, 8:16], spare[:, g, :])
                step(last)
                for g in range(groups):
                    last = V.max_index(where[:, g, 8:16], best[:, g, 8:16], spare[:, g, :])
                step(last)

            def pair_up(dst, first, second):
                for a, na, nb, c in BLOCKS:
                    if na == 1:
                        o, s0, s1 = dst[:, :, c:c + nb], first[:, :, a:a + 1], second[:, :, 0:nb]
                        last = V.tensor_tensor(o, s0.broadcast_to([P, HEADS, nb]), s1, ALU.add)
                    elif nb == 1:
                        o, s0, s1 = dst[:, :, c:c + na], first[:, :, a:a + na], second[:, :, 0:1]
                        last = V.tensor_tensor(o, s0, s1.broadcast_to([P, HEADS, na]), ALU.add)
                    else:
                        o = dst[:, :, c:c + na * nb].rearrange("p g (a b) -> p g a b", b=nb)
                        s0 = first[:, :, a:a + na].unsqueeze(3).broadcast_to([P, HEADS, na, nb])
                        s1 = second[:, :, 0:nb].unsqueeze(2).broadcast_to([P, HEADS, na, nb])
                        last = V.tensor_tensor(o, s0, s1, ALU.add)
                return last

            def select(b, i):
                hs = h[:, b * NT + i, :]

                def residual(_m, o, inv):
                    step(V.tensor_scalar(rinv[:, 1:2], inv, D ** -0.5, None, ALU.mult))
                    step(V.scalar_tensor_tensor(hs, o, rinv[:, 1:2], hs, ALU.mult, ALU.add))

                attend([NT], residual)
                layer_norm(hs)
                dve.wait_ge(sims_copied, 1)
                dve.sem_inc(sims_copied, -1)
                dve.sem_inc(sims_seen, 1)
                top16(sims, sims2, top_v, top_i, 2 * HEADS)
                step(V.tensor_copy(top_f[:], top_i[:]))
                V.tensor_tensor(top_f[:, 0:HEADS, :], top_f[:, 0:HEADS, :],
                                head_off[:].unsqueeze(2).broadcast_to([P, HEADS, TOPK]), ALU.add)
                step(V.tensor_scalar(top_f[:, HEADS:, :], top_f[:, HEADS:, :], float(KEYS), None, ALU.mult))
                pair_up(cand_i, top_f[:, 0:HEADS, :], top_f[:, HEADS:, :])
                step(pair_up(cand_v, top_v[:, 0:HEADS, :], top_v[:, HEADS:, :]))
                top16(cand_v, cand_v2, fin_v, fin_p, HEADS)
                step(V.tensor_copy(fin_f[:], fin_p[:]))
                for g in range(0, HEADS, 2):
                    place = fin_f[:, g:g + 2, :].rearrange("p g r -> p (g r)")
                    step(V.tensor_tensor(hot[:], place.unsqueeze(2).broadcast_to([P, 2 * TOPK, CAND]),
                                         iota_c[:].unsqueeze(1).broadcast_to([P, 2 * TOPK, CAND]), ALU.is_equal))
                    hot4 = hot[:].rearrange("p (g r) c -> p g r c", g=2)
                    step(V.tensor_tensor(hot4, hot4, cand_i[:, g:g + 2, :].unsqueeze(2)
                                         .broadcast_to([P, 2, TOPK, CAND]), ALU.mult))
                    step(V.tensor_reduce(row_f[:, g * TOPK:(g + 2) * TOPK], hot[:], AX.X, ALU.add))
                V.tensor_copy(row_i[:, i, :], row_f[:]).then_inc(rows_chosen, 1)
                step(V.tensor_copy(w_sum[:, 0, :], fin_v[:, :, 0]))
                V.tensor_tensor(fin_v[:], fin_v[:], w_sum[:, 0, :].unsqueeze(2).broadcast_to([P, HEADS, TOPK]),
                                ALU.subtract).then_inc(fin_ready, 1)
                dve.wait_ge(fin_exp, 1)
                dve.sem_inc(fin_exp, -1)
                step(V.tensor_reduce(w_sum[:, 0, :], row_w[:, i, :, :], AX.X, ALU.add))
                step(V.reciprocal(w_sum[:, 1, :], w_sum[:, 0, :]))
                step(V.tensor_tensor(row_w[:, i, :, :], row_w[:, i, :, :],
                                     w_sum[:, 1, :].unsqueeze(2).broadcast_to([P, HEADS, TOPK]), ALU.mult))

            def gather(b, i):
                for g in range(HEADS):
                    use = (HEADS // RING) * i + g // RING + 1
                    dve.wait_ge(rows_landed[g % RING], b * (PER_USE * (HEADS // RING) * NT) + PER_USE * use)
                    dve.sem_inc(rows_seen, 1)
                    dve.wait_ge(rows_seen, 1)
                    dve.sem_inc(rows_seen, -1)
                    slot = rows[:, g % RING, :, :]
                    step(V.tensor_tensor(slot, slot,
                                         row_w[:, i, g, :].unsqueeze(2).broadcast_to([P, TOPK, 2 * D]), ALU.mult))
                    step(V.tensor_reduce(kv[:, i, :, g, :], slot.rearrange("p r (w d) -> p w d r", w=2), AX.X, ALU.add))
                    dve.sem_inc(slot_free[g % RING], 1)
                dve.sem_inc(kv_ready, 1)

            def back(b, i):
                hs = h[:, b * NT + i, :]

                def keep(m, o, inv):
                    last = V.tensor_scalar(cx[:, m * D:(m + 1) * D], o, inv, None, ALU.mult)
                    if m == HEADS - 1:
                        last.then_inc(heads_ready, 1)

                attend([i + 1] * HEADS, keep)
                dve.wait_ge(mem_out_ready, 1)
                dve.sem_inc(mem_out_ready, -1)
                step(V.tensor_tensor(hs, pO[:, 0:D], hs, ALU.add))
                layer_norm(hs)
                dve.wait_ge(qkv1_ready_dve, 1)
                dve.sem_inc(qkv1_ready_dve, -1)
                V.tensor_tensor(v1[:, i, :], pO[:, 0:D], bv[:], ALU.add).then_inc(v1_ready, 1)

                def keep1(_m, o, inv):
                    V.tensor_scalar(cx[:, 0:D], o, inv, None, ALU.mult).then_inc(heads_ready, 1)

                attend([i + 1], keep1)
                step(V.tensor_tensor(hs, hs, bproj[:], ALU.add))
                dve.wait_ge(mem_out_ready, 1)
                dve.sem_inc(mem_out_ready, -1)
                step(V.tensor_tensor(hs, pO[:, 0:D], hs, ALU.add))
                layer_norm(hs)
                dve.wait_ge(logits_ready, 1)
                dve.sem_inc(logits_ready, -1)
                step(V.tensor_tensor(gate[:, 0, :], pM[:, 0:EXPERTS], gb[:], ALU.add))
                step(V.tensor_reduce(rs[:, 6:7], gate[:, 0, :], AX.X, ALU.max))
                V.tensor_scalar(gate[:, 0, :], gate[:, 0, :], rs[:, 6:7], None, ALU.subtract)\
                 .then_inc(logits_shifted, 1)
                dve.wait_ge(gate_exp, 1)
                dve.sem_inc(gate_exp, -1)
                step(V.reciprocal(rs[:, 6:7], w_sum[:, 1, 0:1]))
                step(V.tensor_scalar(gate[:, 2, :], gate[:, 1, :], rs[:, 6:7], None, ALU.mult))
                step(V.max(gate[:, 4, :], gate[:, 2, :]))
                step(V.tensor_copy(gate[:, 5, 0:2], gate[:, 4, 0:2]))
                probs16 = gate[:, 2:4, :].rearrange("p a e -> p (a e)")
                rest16 = gate[:, 6:8, :].rearrange("p a e -> p (a e)")
                step(V.match_replace(rest16, gate[:, 5, :], probs16, 0.0))
                step(V.tensor_tensor(gate[:, 4, :], gate[:, 2, :], gate[:, 6, :], ALU.subtract))
                dve.wait_ge(experts_ready, 1)
                dve.sem_inc(experts_ready, -1)
                y = pO[:].rearrange("p (e d) -> p e d", d=D)
                step(V.tensor_tensor(ysc[:], y, b2_s[:], ALU.add))
                step(V.tensor_tensor(ysc[:], ysc[:], gate[:, 4, :].unsqueeze(2).broadcast_to([P, EXPERTS, D]),
                                     ALU.mult))
                step(V.tensor_reduce(ysum[:], ysc[:].rearrange("p e d -> p d e"), AX.X, ALU.add))
                dve.wait_ge(out_stored, 16)
                dve.sem_inc(out_stored, -16)
                V.tensor_tensor(outt[:], hs, ysum[:], ALU.add).then_inc(out_ready, 1)

            dve.wait_ge(masks_ready_dve, 1)
            dve.sem_inc(masks_ready_dve, -1)
            dve.wait_ge(ids_loaded, 16)
            step(V.tensor_copy(ids_f[:, 0, :], ids_s[:]))
            step(V.tensor_scalar(ids_f[:, 1, :], ids_f[:, 0, :], 0.0, float(VOCAB), ALU.is_lt, ALU.mult))
            step(V.tensor_tensor(ids_f[:, 0, :], ids_f[:, 0, :], ids_f[:, 1, :], ALU.add))
            step(V.tensor_scalar(ids_f[:, 0, :], ids_f[:, 0, :], 0.0, float(VOCAB - 1), ALU.max, ALU.min))
            V.tensor_scalar(ids_u[:], ids_f[:, 0, :], float(PLE_GROUPS), float(PLE_LAYER),
                            ALU.mult, ALU.add).then_inc(text_ids_ready, 1)
            step(V.memset(gate[:, 2:8, :], -1.0))
            dve.wait_ge(w_loaded_dve, 1)
            dve.sem_inc(w_loaded_dve, -1)
            step(V.tensor_tensor(posb[:], posb[:], tokb[:].unsqueeze(1).broadcast_to([P, PT_TILES, D]), ALU.add))
            for g in range(RING):
                dve.sem_inc(slot_free[g], 1)
            dve.sem_inc(out_stored, 16)
            dve.sem_inc(xn_free, 1)
            dve.wait_ge(text_loaded, 16 * BATCH)
            front(0)
            for i in range(NT):
                select(0, i)
            with dve.Fori(0, BATCH - 1) as b:
                front(b + 1)
                for i in range(NT):
                    gather(b, i)
                    back(b, i)
                    select(b + 1, i)
            for i in range(NT):
                gather(BATCH - 1, i)
                back(BATCH - 1, i)


def kernel(**inputs):
    import numpy as np
    import concourse.bacc as bacc
    from concourse.bass_utils import run_bass_kernel_spmd

    a = {k: np.asarray(v) for k, v in inputs.items()}
    arrays = {
        "x": a["x"], "ids": a["x_txt"].T,
        "tok_wT": a["L0_tok_W"].T, "tok_b": a["L0_tok_b"], "pos": a["L0_tok_pos_embed"][0],
        "ple": a["L0_txt_ple_table"].reshape(VOCAB * PLE_GROUPS, D),
        "wqT": a["L0_attn_Wq"].T, "wkT": a["L0_attn_Wk"].T, "wvT": a["L0_attn_Wv"].T,
        "wq_pk": a["L0_ffn_Wq_pk"], "keysT": a["L0_ffn_pk_keys"].transpose(0, 2, 3, 1),
        "wq_mem": a["L0_ffn_Wq"],
        "kv_table": np.concatenate([a["L0_ffn_keys_table"], a["L0_ffn_values_table"]], axis=1),
        "wo": a["L0_ffn_Wo"], "w_qkv": a["L1_attn_W_qkv"], "b_qkv": a["L1_attn_b_qkv"],
        "w_proj": a["L1_attn_W_proj"], "b_proj": a["L1_attn_b_proj"],
        "gate_w": a["L1_ffn_gate_w"], "gate_b": a["L1_ffn_gate_b"],
        "w1": a["L1_ffn_W1"], "b1T": a["L1_ffn_b1"].T, "w2": a["L1_ffn_W2"], "b2": a["L1_ffn_b2"],
    }
    arrays = {k: np.ascontiguousarray(v) for k, v in arrays.items()}
    nc = bacc.Bacc("TRN2", target_bir_lowering=False, num_devices=1)
    args = {k: nc.dram_tensor(k, v.shape, mybir.dt.from_np(v.dtype), kind="ExternalInput").ap()
            for k, v in arrays.items()}
    out = nc.dram_tensor("out", (BATCH, TOKENS, D), F32, kind="ExternalOutput").ap()
    build(nc, out=out, **args)
    result = run_bass_kernel_spmd(nc, [arrays], core_ids=[0])
    return result.results[0]["out"]
```

```python
from contextlib import ExitStack

import concourse.bass as bass
from concourse import mybir

F32 = mybir.dt.float32
BF16 = mybir.dt.bfloat16
I32 = mybir.dt.int32
U32 = mybir.dt.uint32
ALU = mybir.AluOpType
ACT = mybir.ActivationFunctionType
AX = mybir.AxisListType

P = 128
BATCH, MELS, FRAMES, PATCH = 4, 128, 512, 8
D = 64
PATCHES = (MELS // PATCH) * (FRAMES // PATCH)
TEXT = 128
TOKENS = PATCHES + TEXT
NT = TOKENS // P
PT_TILES = PATCHES // P
FJ = FRAMES // PATCH
VOCAB, PLE_GROUPS, PLE_LAYER = 32000, 8, 3
HEADS, KEYS, DK, TOPK = 8, 64, 32, 16
SLOTS = KEYS * KEYS
RING = 4
EXPERTS, HID = 8, 128
EPS = 1e-5
BANK = 512
LOWEST = -3.4028234663852886e38
MASKED = -1e30
PER_USE = 16 * TOPK
RSQRT_SEED = float(0x5F3759DF)
LEAD = 3
ATTEND = 2
BACK = 1 + ATTEND * HEADS + 3 + ATTEND + 5
SELECT = ATTEND + 2 + 12
FRONT = 3 * NT
ROWS = [(a, TOPK // (a + 1)) for a in range(TOPK)]
CAND = sum(n for _, n in ROWS)
BLOCKS = []
_col = 0
for _a, _n in ROWS:
    if BLOCKS and BLOCKS[-1][2] == _n:
        BLOCKS[-1][1] += 1
    else:
        BLOCKS.append([_a, 1, _n, _col])
    _col += _n


def order(*lengths):
    spots = [((k + 0.5) / n, chain) for chain, n in enumerate(lengths) for k in range(n)]
    return [chain for _, chain in sorted(spots)]


def run(chains, lengths):
    for chain in order(*lengths):
        if chains[chain] is not None:
            next(chains[chain])
    for c in chains:
        assert c is None or next(c, None) is None


def chain_of(*chains):
    for c in chains:
        yield from c


def tile_spot(j):
    return (3 * BANK + j * P) if j < 4 else (BANK + (j - 4) * P)


class Scratch:
    pass


def build(nc, x_in, ids, tok_wT, tok_b, pos, ple, wqT, wkT, wvT, wq_pk, keysT, wq_mem, kv_table, wo,
          w_qkv, b_qkv, w_proj, b_proj, gate_w, gate_b, w1, b1T, w2, b2, out):
    ctx = ExitStack()
    with ctx:
        def sb(name, shape, dt=F32):
            return ctx.enter_context(nc.sbuf_tensor(name, shape, dt))

        def ps(name, shape, dt=F32):
            return ctx.enter_context(nc.psum_tensor(name, shape, dt))

        def sem(name):
            return ctx.enter_context(nc.semaphore(name))

        ident = sb("ident", [P, P])
        ident_h = sb("ident_h", [P, P], BF16)
        causal = sb("causal", [P, P], BF16)
        iota_c = sb("iota_c", [P, CAND])
        head_off = sb("head_off", [P, HEADS])
        tokw = sb("tokw", [D, D])
        posb = sb("posb", [P, PT_TILES, D])
        tokb = sb("tokb", [P, D])
        w0 = sb("w0", [D, 3, D])
        wpk = sb("wpk", [D, 2 * HEADS * DK])
        keys_bd = sb("keys_bd", [P, 4, 4 * KEYS])
        wqm = sb("wqm", [D, HEADS * D])
        wo_s = sb("wo_s", [P, 4, D])
        wqkv = sb("wqkv", [D, 3 * D])
        bq = sb("bq", [D, 2])
        bq8 = sb("bq8", [D, 1])
        bv = sb("bv", [P, D])
        wproj = sb("wproj", [D, D])
        bproj = sb("bproj", [P, D])
        gw = sb("gw", [D, EXPERTS])
        gb = sb("gb", [P, EXPERTS])
        w1_s = sb("w1_s", [D, EXPERTS, HID])
        b1_s = sb("b1_s", [HID, EXPERTS])
        w2_s = sb("w2_s", [HID, EXPERTS, D])
        b2_s = sb("b2_s", [P, EXPERTS, D])
        ids_s = sb("ids_s", [P, BATCH], I32)
        ids_f = sb("ids_f", [P, 2, BATCH])
        ids_u = sb("ids_u", [P, BATCH], U32)
        text = sb("text", [P, BATCH, D])

        h = sb("h", [P, BATCH * NT, D])
        patch = sb("patch", [P, PT_TILES, D])
        patchT = sb("patchT", [D, P])
        qk0 = sb("qk0", [D, 2, TOKENS])
        v0 = sb("v0", [P, NT, D])
        xn2T = sb("xn2T", [D, NT, P])
        qpkT = sb("qpkT", [P, BANK])
        sims = sb("sims", [P, 2 * HEADS, KEYS])
        sims2 = sb("sims2", [P, 2 * HEADS, KEYS])
        top_v = sb("top_v", [P, 2 * HEADS, TOPK])
        top_i = sb("top_i", [P, 2 * HEADS, TOPK], U32)
        top_f = sb("top_f", [P, 2 * HEADS, TOPK])
        cand_v = sb("cand_v", [P, HEADS, CAND])
        cand_v2 = sb("cand_v2", [P, HEADS, CAND])
        cand_i = sb("cand_i", [P, HEADS, CAND])
        fin_v = sb("fin_v", [P, HEADS, TOPK])
        fin_p = sb("fin_p", [P, HEADS, TOPK], U32)
        fin_f = sb("fin_f", [P, HEADS, TOPK])
        hot = sb("hot", [P, 2 * TOPK, CAND])
        row_f = sb("row_f", [P, HEADS * TOPK])
        w_sum = sb("w_sum", [P, 2, HEADS])
        row_i = sb("row_i", [P, NT, HEADS * TOPK], U32)
        row_w = sb("row_w", [P, NT, HEADS, TOPK])
        rows = sb("rows", [P, RING, TOPK, 2 * D])
        kv = sb("kv", [P, 2, HEADS, D])
        kT = sb("kT", [P, 4, TOKENS])
        vm = sb("vm", [P, NT, HEADS * D])
        qmT = sb("qmT", [P, BANK])
        cx = sb("cx", [P, BANK])
        cxT = sb("cxT", [P, BANK])
        q1T = sb("q1T", [D, P])
        k1T = sb("k1T", [D, TOKENS])
        v1 = sb("v1", [P, NT, D])
        gate = sb("gate", [P, 8, EXPERTS])
        gate_sum = sb("gate_sum", [P, 2])
        gelT = sb("gelT", [HID, EXPERTS, P])
        ysc = sb("ysc", [P, EXPERTS, D])
        ysum = sb("ysum", [P, D])
        outt = sb("outt", [P, D])

        def scratch(n):
            t = Scratch()
            t.ps = ps(f"{n}_ps", [P, 4 * BANK])
            t.O = t.ps[:, 0:BANK]
            t.M = t.ps[:, 3 * BANK:4 * BANK]
            t.st6 = sb(f"{n}_st6", [P, 6])
            t.mv = sb(f"{n}_mv", [P, 2])
            t.rs = sb(f"{n}_rs", [P, 8])
            t.rsi = sb(f"{n}_rsi", [P, 2], I32)
            t.xn = sb(f"{n}_xn", [P, D])
            t.xnT = sb(f"{n}_xnT", [D, P])
            t.probs = sb(f"{n}_probs", [P, TOKENS])
            t.probsT = sb(f"{n}_probsT", [P, TOKENS])
            t.nmax = sb(f"{n}_nmax", [P, 1])
            t.rsum = sb(f"{n}_rsum", [P, 1])
            t.rinv = sb(f"{n}_rinv", [P, 1])
            t.xn_ready = sem(f"{n}_xn_ready")
            t.xn_free = sem(f"{n}_xn_free")
            t.xnT_ready = sem(f"{n}_xnT_ready")
            t.xnT_copied = sem(f"{n}_xnT_copied")
            t.scores_ready = sem(f"{n}_scores_ready")
            t.negmax_ready = sem(f"{n}_negmax_ready")
            t.probs_ready = sem(f"{n}_probs_ready")
            t.probsT_ready = sem(f"{n}_probsT_ready")
            t.probsT_copied = sem(f"{n}_probsT_copied")
            t.ctx_ready = sem(f"{n}_ctx_ready")
            t.ctx_read = sem(f"{n}_ctx_read")
            return t

        x, y = scratch("back"), scratch("select")

        const_loaded = sem("const_loaded")
        w_loaded_pe = sem("w_loaded_pe")
        w_loaded_act = sem("w_loaded_act")
        w_loaded_dve = sem("w_loaded_dve")
        keys_zeroed = sem("keys_zeroed")
        keys_loaded = sem("keys_loaded")
        ids_loaded = sem("ids_loaded")
        pool_step = sem("pool_step")
        masks_ready = sem("masks_ready")
        masks_ready_dve = sem("masks_ready_dve")
        text_ids_ready = sem("text_ids_ready")
        text_loaded = sem("text_loaded")
        bq8_ready = sem("bq8_ready")
        patch_loaded = sem("patch_loaded")
        patch_free = sem("patch_free")
        dve_step = sem("dve_step")
        patchT_ready = sem("patchT_ready")
        patchT_copied = sem("patchT_copied")
        emb_ready = sem("emb_ready")
        qkv0_ready = sem("qkv0_ready")
        qkv0_copied = sem("qkv0_copied")
        qpk_ready = sem("qpk_ready")
        qpk_copied = sem("qpk_copied")
        sims_ready = sem("sims_ready")
        sims_copied = sem("sims_copied")
        sims_seen = sem("sims_seen")
        fin_ready = sem("fin_ready")
        fin_exp = sem("fin_exp")
        rows_chosen = sem("rows_chosen")
        rows_landed = [sem(f"rows_landed{n}") for n in range(RING)]
        rows_seen = sem("rows_seen")
        slot_free = [sem(f"slot_free{n}") for n in range(RING)]
        kv_ready = sem("kv_ready")
        kv_free = sem("kv_free")
        kq_ready = sem("kq_ready")
        kq_copied = sem("kq_copied")
        heads_ready = sem("heads_ready")
        headsT_ready = sem("headsT_ready")
        headsT_copied = sem("headsT_copied")
        mem_out_ready = sem("mem_out_ready")
        qkv1_ready = sem("qkv1_ready")
        qkv1_ready_dve = sem("qkv1_ready_dve")
        qk1_copied = sem("qk1_copied")
        v1_ready = sem("v1_ready")
        logits_ready = sem("logits_ready")
        logits_shifted = sem("logits_shifted")
        gate_exp = sem("gate_exp")
        hidden_ready = sem("hidden_ready")
        gelu_ready = sem("gelu_ready")
        experts_ready = sem("experts_ready")
        experts_read = sem("experts_read")
        out_ready = sem("out_ready")
        out_stored = sem("out_stored")

        block = ctx.enter_context(nc.Block())

        @block.sync
        def _(sp):
            sp.dma_start(ids_s[:], ids).then_inc(ids_loaded, 16)

            def load_patches(b):
                for m in range(MELS // PATCH):
                    src = x_in[b, 0, m * PATCH:(m + 1) * PATCH, :].rearrange("p (j f) -> j p f", f=PATCH)
                    dst = patch[FJ * (m % 2):FJ * (m % 2) + FJ, m // 2, :].rearrange("j (p f) -> j p f", f=PATCH)
                    sp.dma_start(dst, src).then_inc(patch_loaded, 16)

            load_patches(0)
            loads = [
                (tokw[:], tok_wT), (posb[:], pos.rearrange("(t p) e -> p t e", p=P)),
                (tokb[:], tok_b.partition_broadcast(P)),
                (w0[:, 0, :], wqT), (w0[:, 1, :], wkT), (w0[:, 2, :], wvT),
                (wpk[:], wq_pk), (wqm[:], wq_mem), (wo_s[:], wo.rearrange("(c p) e -> p c e", p=P)),
                (wqkv[:], w_qkv), (bq[:, 0:1], b_qkv[0:D].unsqueeze(1)), (bq[:, 1:2], b_qkv[D:2 * D].unsqueeze(1)),
                (bv[:], b_qkv[2 * D:3 * D].partition_broadcast(P)),
                (wproj[:], w_proj), (bproj[:], b_proj.partition_broadcast(P)),
                (gw[:], gate_w), (gb[:], gate_b.partition_broadcast(P)),
                (w1_s[:], w1.rearrange("e d k -> d e k")),
                (b1_s[:], b1T), (w2_s[:], w2.rearrange("e k d -> k e d")),
                (b2_s[:].rearrange("p e d -> p (e d)"), b2.rearrange("e d -> (e d)").partition_broadcast(P)),
            ]
            for dst, src in loads:
                sp.dma_start(dst, src).then_inc(const_loaded, 16)
            sp.wait_ge(const_loaded, 16 * len(loads))
            for s in (w_loaded_pe, w_loaded_act, w_loaded_dve):
                sp.sem_inc(s, 1)
            sp.wait_ge(keys_zeroed, 1)
            for p in range(2):
                for g in range(HEADS):
                    r = DK * (g % 4)
                    sp.dma_start(keys_bd[r:r + DK, 2 * p + g // 4, KEYS * (g % 4):KEYS * (g % 4) + KEYS],
                                 keysT[p, g]).then_inc(keys_loaded, 16)
            for b in range(1, BATCH):
                sp.wait_ge(patch_free, 1)
                sp.sem_inc(patch_free, -1)
                load_patches(b)

        @block.gpsimd
        def _(pool):
            def step(ins):
                ins.then_inc(pool_step, 1)
                pool.wait_ge(pool_step, 1)
                pool.sem_inc(pool_step, -1)

            pool.memset(keys_bd[:], 0.0).then_inc(keys_zeroed, 1)
            step(pool.memset(ident[:], 0.0))
            step(pool.affine_select(out=ident[:], in_=ident[:], compare_op=ALU.not_equal, fill=1.0, base=0,
                                    pattern=[[-1, P]], channel_multiplier=1))
            step(pool.tensor_copy(ident_h[:], ident[:]))
            step(pool.memset(causal[:], 0.0))
            step(pool.affine_select(out=causal[:], in_=causal[:], compare_op=ALU.is_ge, fill=MASKED, base=0,
                                    pattern=[[-1, P]], channel_multiplier=1))
            step(pool.iota(iota_c[:], pattern=[[1, CAND]], base=0, channel_multiplier=0,
                           allow_small_or_imprecise_dtypes=True))
            step(pool.iota(head_off[:], pattern=[[SLOTS, HEADS]], base=0, channel_multiplier=0,
                           allow_small_or_imprecise_dtypes=True))
            pool.sem_inc(masks_ready, 1)
            pool.sem_inc(masks_ready_dve, 1)
            pool.wait_ge(text_ids_ready, 1)
            pool.sem_inc(text_ids_ready, -1)
            for b in range(BATCH):
                pool.indirect_dma_start(
                    out=text[:, b, :], out_offset=None, in_=ple,
                    in_offset=bass.IndirectOffsetOnAxis(ap=ids_u[:, b:b + 1], axis=0)).then_inc(text_loaded, 16)

            with pool.Fori(0, BATCH) as _b:
                for i in range(NT):
                    pool.wait_ge(rows_chosen, 1)
                    pool.sem_inc(rows_chosen, -1)
                    for g in range(HEADS):
                        pool.wait_ge(slot_free[g % RING], 1)
                        pool.sem_inc(slot_free[g % RING], -1)
                        for r in range(TOPK):
                            c = g * TOPK + r
                            pool.indirect_dma_start(
                                out=rows[:, g % RING, r, :], out_offset=None, in_=kv_table,
                                in_offset=bass.IndirectOffsetOnAxis(ap=row_i[:, i, c:c + 1], axis=0),
                            ).then_inc(rows_landed[g % RING], 16)

        @block.tensor
        def _(pe):
            mm = nc.tensor.matmul

            def transpose_xn(t):
                pe.wait_ge(t.xn_ready, 1)
                pe.sem_inc(t.xn_ready, -1)
                nc.tensor.transpose(t.M[0:D, 0:P], t.xn[:], ident[:]).then_inc(t.xnT_ready, 1)
                pe.wait_ge(t.xnT_copied, 1)
                pe.sem_inc(t.xnT_copied, -1)
                pe.sem_inc(t.xn_free, 1)

            def attend(t, q, k, v, n, masked):
                for c in range(0, n * P, BANK):
                    e = min(c + BANK, n * P)
                    diag = masked and e == n * P
                    last = mm(t.ps[:, c:e], q, k[:, c:e], start=True, stop=not diag)
                    if diag:
                        last = mm(t.ps[:, e - P:e], ident_h[:], causal[:], start=False, stop=True)
                last.then_inc(t.scores_ready, 1)
                yield
                pe.wait_ge(t.probs_ready, 1)
                pe.sem_inc(t.probs_ready, -1)
                for j0 in range(0, n, 4):
                    for j in range(j0, min(j0 + 4, n)):
                        o = tile_spot(j)
                        last = nc.tensor.transpose(t.ps[:, o:o + P], t.probs[:, j * P:(j + 1) * P], ident[:])
                    last.then_inc(t.probsT_ready, 1)
                for j0 in range(0, n, 4):
                    pe.wait_ge(t.probsT_copied, 1)
                    pe.sem_inc(t.probsT_copied, -1)
                    for j in range(j0, min(j0 + 4, n)):
                        last = mm(t.O[:, 0:D], t.probsT[:, j * P:(j + 1) * P], v(j), start=(j == 0), stop=(j == n - 1))
                last.then_inc(t.ctx_ready, 1)
                yield

            def front():
                for i in range(NT):
                    if i < PT_TILES:
                        if i == 0:
                            pe.wait_ge(patch_loaded, 16 * (MELS // PATCH))
                            pe.sem_inc(patch_loaded, -(16 * (MELS // PATCH)))
                        nc.tensor.transpose(y.M[0:D, 0:P], patch[:, i, :], ident[:]).then_inc(patchT_ready, 1)
                        pe.wait_ge(patchT_copied, 1)
                        pe.sem_inc(patchT_copied, -1)
                        mm(y.O[:, 0:D], patchT[:], tokw[:], start=True, stop=True).then_inc(emb_ready, 1)
                        if i == PT_TILES - 1:
                            pe.sem_inc(patch_free, 1)
                    yield
                    yield
                    transpose_xn(y)
                    mm(y.M[0:D, 0:P], w0[:, 0, :], y.xnT[:], start=True, stop=True)
                    mm(y.M[0:D, P:2 * P], w0[:, 1, :], y.xnT[:], start=True, stop=True)
                    mm(y.M[:, 2 * P:2 * P + D], y.xnT[:], w0[:, 2, :], start=True, stop=True).then_inc(qkv0_ready, 1)
                    pe.wait_ge(qkv0_copied, 1)
                    pe.sem_inc(qkv0_copied, -1)
                    yield

            def select(i):
                yield from attend(y, qk0[:, 0, i * P:(i + 1) * P], qk0[:, 1, :], lambda j: v0[:, j, :], NT, False)
                yield
                transpose_xn(y)
                for c in range(4):
                    last = mm(y.M[:, c * P:(c + 1) * P], wpk[:, c * P:(c + 1) * P], xn2T[:, i, :], start=True, stop=True)
                last.then_inc(qpk_ready, 1)
                pe.wait_ge(qpk_copied, 1)
                pe.sem_inc(qpk_copied, -1)
                for c in range(4):
                    last = mm(y.ps[:, c * 256:(c + 1) * 256], qpkT[:, c * P:(c + 1) * P], keys_bd[:, c, :],
                              start=True, stop=True)
                last.then_inc(sims_ready, 1)
                yield
                pe.wait_ge(sims_seen, 1)
                pe.sem_inc(sims_seen, -1)
                for _ in range(12):
                    yield

            def back(i):
                pe.wait_ge(kv_ready, 1)
                pe.sem_inc(kv_ready, -1)
                for c in range(4):
                    nc.tensor.transpose(x.O[:, c * P:(c + 1) * P], kv[:, 0, 2 * c:2 * c + 2, :].rearrange(
                        "p g d -> p (g d)"), ident[:])
                for c in range(4):
                    last = mm(x.M[:, c * P:(c + 1) * P], wqm[:, c * P:(c + 1) * P], xn2T[:, i, :], start=True, stop=True)
                last.then_inc(kq_ready, 1)
                pe.wait_ge(kq_copied, 1)
                pe.sem_inc(kq_copied, -1)
                yield
                for g in range(HEADS):
                    r = D * (g % 2)
                    yield from attend(x, qmT[r:r + D, (g // 2) * P:(g // 2 + 1) * P], kT[r:r + D, g // 2, :],
                                      lambda j, g=g: vm[:, j, g * D:(g + 1) * D], i + 1, True)
                    pe.wait_ge(x.ctx_read, 1)
                    pe.sem_inc(x.ctx_read, -1)
                for c in range(4):
                    last = nc.tensor.transpose(x.M[:, c * P:(c + 1) * P], cx[:, c * P:(c + 1) * P], ident[:])
                last.then_inc(headsT_ready, 1)
                pe.wait_ge(headsT_copied, 1)
                pe.sem_inc(headsT_copied, -1)
                for c in range(4):
                    last = mm(x.O[:, 0:D], cxT[:, c * P:(c + 1) * P], wo_s[:, c, :], start=(c == 0), stop=(c == 3))
                last.then_inc(mem_out_ready, 1)
                yield
                yield
                transpose_xn(x)
                mm(x.M[0:D, 0:P], wqkv[:, 0:D], x.xnT[:], start=True, stop=True)
                mm(x.M[0:D, P:2 * P], wqkv[:, D:2 * D], x.xnT[:], start=True, stop=True).then_inc(qkv1_ready, 1)
                mm(x.O[:, 0:D], x.xnT[:], wqkv[:, 2 * D:3 * D], start=True, stop=True).then_inc(qkv1_ready_dve, 1)
                pe.wait_ge(qk1_copied, 1)
                pe.sem_inc(qk1_copied, -1)
                pe.wait_ge(v1_ready, 1)
                pe.sem_inc(v1_ready, -1)
                yield
                yield from attend(x, q1T[:], k1T[:], lambda j: v1[:, j, :], i + 1, True)
                pe.wait_ge(x.ctx_read, 1)
                pe.sem_inc(x.ctx_read, -1)
                nc.tensor.transpose(x.M[0:D, 0:P], cx[:, 0:D], ident[:]).then_inc(headsT_ready, 1)
                pe.wait_ge(headsT_copied, 1)
                pe.sem_inc(headsT_copied, -1)
                mm(x.O[:, 0:D], cxT[0:D, 0:P], wproj[:], start=True, stop=True).then_inc(mem_out_ready, 1)
                yield
                yield
                transpose_xn(x)
                mm(x.M[:, 0:EXPERTS], x.xnT[:], gw[:], start=True, stop=True).then_inc(logits_ready, 1)
                for e in range(EXPERTS):
                    last = mm(x.ps[:, BANK + e * P:BANK + (e + 1) * P], w1_s[:, e, :], x.xnT[:], start=True, stop=True)
                last.then_inc(hidden_ready, 1)
                yield
                pe.wait_ge(gelu_ready, 1)
                pe.sem_inc(gelu_ready, -1)
                for e in range(EXPERTS):
                    last = mm(x.O[:, e * D:(e + 1) * D], gelT[:, e, :], w2_s[:, e, :], start=True, stop=True)
                last.then_inc(experts_ready, 1)
                yield
                pe.wait_ge(experts_read, 1)
                pe.sem_inc(experts_read, -1)
                yield

            pe.wait_ge(masks_ready, 1)
            pe.sem_inc(masks_ready, -1)
            pe.wait_ge(w_loaded_pe, 1)
            pe.sem_inc(w_loaded_pe, -1)
            for _ in front():
                pass
            pe.wait_ge(keys_loaded, 16 * 2 * HEADS)
            for i in range(LEAD):
                for _ in select(i):
                    pass
            with pe.Fori(0, BATCH - 1):
                for i in range(NT):
                    if i + LEAD < NT:
                        run((back(i), None, select(i + LEAD)), (BACK, HEADS, SELECT))
                    elif i + LEAD == NT:
                        run((back(i), None, chain_of(front(), select(0))), (BACK, HEADS, FRONT + SELECT))
                    else:
                        run((back(i), None, select(i + LEAD - NT)), (BACK, HEADS, SELECT))
            for i in range(NT):
                if i + LEAD < NT:
                    run((back(i), None, select(i + LEAD)), (BACK, HEADS, SELECT))
                elif i < NT - 1:
                    run((back(i), None), (BACK, HEADS))
                else:
                    run((back(i),), (BACK,))

        @block.scalar
        def _(act):
            def copy(dst, src, done, scale=1.0):
                nc.scalar.activation(dst, src, ACT.Copy, scale=scale).then_inc(done, 1)

            def copy_xnT(t, dst):
                act.wait_ge(t.xnT_ready, 1)
                act.sem_inc(t.xnT_ready, -1)
                copy(dst, t.M[0:D, 0:P], t.xnT_copied)

            def attend(t, n):
                yield
                act.wait_ge(t.negmax_ready, 1)
                act.sem_inc(t.negmax_ready, -1)
                nc.scalar.activation(t.probs[:, 0:n * P], t.ps[:, 0:n * P], ACT.Exp, bias=t.nmax[:],
                                     accum_out=t.rsum[:]).then_inc(t.probs_ready, 1)
                for j in range(0, n, 4):
                    act.wait_ge(t.probsT_ready, 1)
                    act.sem_inc(t.probsT_ready, -1)
                    o, m = tile_spot(j), min(4, n - j) * P
                    copy(t.probsT[:, j * P:j * P + m], t.ps[:, o:o + m], t.probsT_copied)
                yield

            def front():
                for i in range(NT):
                    if i < PT_TILES:
                        act.wait_ge(patchT_ready, 1)
                        act.sem_inc(patchT_ready, -1)
                        copy(patchT[:], y.M[0:D, 0:P], patchT_copied)
                    yield
                    yield
                    copy_xnT(y, y.xnT[:])
                    act.wait_ge(qkv0_ready, 1)
                    act.sem_inc(qkv0_ready, -1)
                    nc.scalar.activation(qk0[:, :, i * P:(i + 1) * P],
                                         y.M[0:D, 0:2 * P].rearrange("d (w t) -> d w t", w=2), ACT.Copy)
                    copy(v0[:, i, :], y.M[:, 2 * P:2 * P + D], qkv0_copied)
                    yield

            def select(i):
                yield from attend(y, NT)
                yield
                copy_xnT(y, xn2T[:, i, :])
                act.wait_ge(qpk_ready, 1)
                act.sem_inc(qpk_ready, -1)
                copy(qpkT[:], y.M, qpk_copied)
                act.wait_ge(sims_ready, 1)
                act.sem_inc(sims_ready, -1)
                copy(sims[:].rearrange("p g k -> p (g k)"), y.ps[:, 0:2 * HEADS * KEYS], sims_copied)
                yield
                for _ in range(11):
                    yield
                act.wait_ge(fin_ready, 1)
                act.sem_inc(fin_ready, -1)
                nc.scalar.activation(row_w[:, i, :, :], fin_v[:], ACT.Exp).then_inc(fin_exp, 1)
                yield

            def back(b, i):
                act.wait_ge(kq_ready, 1)
                act.sem_inc(kq_ready, -1)
                nc.scalar.activation(kT[:, :, i * P:(i + 1) * P],
                                     x.O.rearrange("p (c t) -> p c t", c=4), ACT.Copy)
                copy(vm[:, i, :], kv[:, 1, :, :].rearrange("p g d -> p (g d)"), kv_free)
                copy(qmT[:], x.M, kq_copied, scale=D ** -0.5)
                yield
                for g in range(HEADS):
                    yield from attend(x, i + 1)
                act.wait_ge(headsT_ready, 1)
                act.sem_inc(headsT_ready, -1)
                copy(cxT[:], x.M, headsT_copied)
                yield
                yield
                copy_xnT(x, x.xnT[:])
                act.wait_ge(qkv1_ready, 1)
                act.sem_inc(qkv1_ready, -1)
                nc.scalar.activation(q1T[:], x.M[0:D, 0:P], ACT.Identity, bias=bq8[:], scale=D ** -0.5)
                nc.scalar.activation(k1T[:, i * P:(i + 1) * P], x.M[0:D, P:2 * P], ACT.Identity,
                                     bias=bq[:, 1:2]).then_inc(qk1_copied, 1)
                yield
                yield from attend(x, i + 1)
                act.wait_ge(headsT_ready, 1)
                act.sem_inc(headsT_ready, -1)
                copy(cxT[0:D, 0:P], x.M[0:D, 0:P], headsT_copied)
                yield
                yield
                copy_xnT(x, x.xnT[:])
                act.wait_ge(logits_shifted, 1)
                act.sem_inc(logits_shifted, -1)
                nc.scalar.activation(gate[:, 1, :], gate[:, 0, :], ACT.Exp,
                                     accum_out=gate_sum[:, 0:1]).then_inc(gate_exp, 1)
                yield
                act.wait_ge(hidden_ready, 1)
                act.sem_inc(hidden_ready, -1)
                for e in range(EXPERTS):
                    last = nc.scalar.activation(gelT[:, e, :], x.ps[:, BANK + e * P:BANK + (e + 1) * P], ACT.Gelu,
                                                bias=b1_s[:, e:e + 1])
                last.then_inc(gelu_ready, 1)
                yield
                act.wait_ge(out_ready, 1)
                act.sem_inc(out_ready, -1)
                act.dma_start(out[b, i * P:(i + 1) * P, :], outt[:]).then_inc(out_stored, 16)
                yield

            act.wait_ge(w_loaded_act, 1)
            act.sem_inc(w_loaded_act, -1)
            nc.scalar.activation(bq8[:], bq[:, 0:1], ACT.Copy, scale=D ** -0.5).then_inc(bq8_ready, 1)
            act.wait_ge(bq8_ready, 1)
            act.sem_inc(bq8_ready, -1)
            for _ in front():
                pass
            for i in range(LEAD):
                for _ in select(i):
                    pass
            with act.Fori(0, BATCH - 1) as b:
                for i in range(NT):
                    if i + LEAD < NT:
                        run((back(b, i), None, select(i + LEAD)), (BACK, HEADS, SELECT))
                    elif i + LEAD == NT:
                        run((back(b, i), None, chain_of(front(), select(0))), (BACK, HEADS, FRONT + SELECT))
                    else:
                        run((back(b, i), None, select(i + LEAD - NT)), (BACK, HEADS, SELECT))
            for i in range(NT):
                if i + LEAD < NT:
                    run((back(BATCH - 1, i), None, select(i + LEAD)), (BACK, HEADS, SELECT))
                elif i < NT - 1:
                    run((back(BATCH - 1, i), None), (BACK, HEADS))
                else:
                    run((back(BATCH - 1, i),), (BACK,))
            act.wait_ge(out_stored, 16)

        @block.vector
        def _(dve):
            V = nc.vector

            def step(ins):
                ins.then_inc(dve_step, 1)
                dve.wait_ge(dve_step, 1)
                dve.sem_inc(dve_step, -1)

            def layer_norm(t, src):
                rs = t.rs
                step(V.bn_stats(t.st6[:], src))
                step(V.bn_aggr(t.mv[:], t.st6[:]))
                step(V.tensor_scalar(rs[:, 0:1], t.mv[:, 1:2], EPS, None, ALU.add))
                V.tensor_scalar(rs[:, 1:2], rs[:, 0:1], 0.5, None, ALU.mult)
                step(V.tensor_scalar(t.rsi[:, 0:1], rs[:, 0:1].bitcast(I32), 1, None, ALU.logical_shift_right))
                step(V.tensor_scalar(rs[:, 2:3].bitcast(I32), t.rsi[:, 0:1], -1.0, RSQRT_SEED, ALU.mult, ALU.add))
                r = 2
                for _ in range(3):
                    step(V.scalar_tensor_tensor(rs[:, 4:5], rs[:, r:r + 1], rs[:, 1:2], rs[:, r:r + 1],
                                                ALU.mult, ALU.mult))
                    step(V.scalar_tensor_tensor(rs[:, 5 - r:6 - r], rs[:, 4:5], 1.5, rs[:, r:r + 1],
                                                ALU.subtract, ALU.mult, reverse0=True))
                    r = 5 - r
                dve.wait_ge(t.xn_free, 1)
                dve.sem_inc(t.xn_free, -1)
                V.tensor_scalar(t.xn[:], src, t.mv[:, 0:1], rs[:, r:r + 1], ALU.subtract, ALU.mult)\
                 .then_inc(t.xn_ready, 1)

            def attend(t, n):
                dve.wait_ge(t.scores_ready, 1)
                dve.sem_inc(t.scores_ready, -1)
                V.tensor_reduce(t.nmax[:], t.ps[:, 0:n * P], AX.X, ALU.max, negate=True).then_inc(t.negmax_ready, 1)
                yield
                yield
                dve.wait_ge(t.ctx_ready, 1)
                dve.sem_inc(t.ctx_ready, -1)
                step(V.reciprocal(t.rinv[:], t.rsum[:]))

            def front(b):
                for i in range(NT):
                    hs = h[:, b * NT + i, :]
                    yield
                    if i < PT_TILES:
                        dve.wait_ge(emb_ready, 1)
                        dve.sem_inc(emb_ready, -1)
                        step(V.tensor_tensor(hs, y.O[:, 0:D], posb[:, i, :], ALU.add))
                    else:
                        step(V.tensor_copy(hs, text[:, b, :]))
                    layer_norm(y, hs)
                    yield
                    yield

            def top16(values, spare, best, where, groups):
                for g in groups:
                    last = V.max(best[:, g, 0:8], values[:, g, :])
                step(last)
                for g in groups:
                    V.max_index(where[:, g, 0:8], best[:, g, 0:8], values[:, g, :])
                    last = V.match_replace(spare[:, g, :], best[:, g, 0:8], values[:, g, :], LOWEST)
                step(last)
                for g in groups:
                    last = V.max(best[:, g, 8:16], spare[:, g, :])
                step(last)
                for g in groups:
                    last = V.max_index(where[:, g, 8:16], best[:, g, 8:16], spare[:, g, :])
                step(last)

            def pair_up(dst, first, second):
                for a, na, nb, c in BLOCKS:
                    if na == 1:
                        o, s0, s1 = dst[:, :, c:c + nb], first[:, :, a:a + 1], second[:, :, 0:nb]
                        last = V.tensor_tensor(o, s0.broadcast_to([P, HEADS, nb]), s1, ALU.add)
                    elif nb == 1:
                        o, s0, s1 = dst[:, :, c:c + na], first[:, :, a:a + na], second[:, :, 0:1]
                        last = V.tensor_tensor(o, s0, s1.broadcast_to([P, HEADS, na]), ALU.add)
                    else:
                        o = dst[:, :, c:c + na * nb].rearrange("p g (a b) -> p g a b", b=nb)
                        s0 = first[:, :, a:a + na].unsqueeze(3).broadcast_to([P, HEADS, na, nb])
                        s1 = second[:, :, 0:nb].unsqueeze(2).broadcast_to([P, HEADS, na, nb])
                        last = V.tensor_tensor(o, s0, s1, ALU.add)
                return last

            def select(b, i):
                hs = h[:, b * NT + i, :]
                yield from attend(y, NT)
                step(V.tensor_scalar(y.rinv[:], y.rinv[:], D ** -0.5, None, ALU.mult))
                step(V.scalar_tensor_tensor(hs, y.O[:, 0:D], y.rinv[:], hs, ALU.mult, ALU.add))
                layer_norm(y, hs)
                yield
                yield
                dve.wait_ge(sims_copied, 1)
                dve.sem_inc(sims_copied, -1)
                dve.sem_inc(sims_seen, 1)
                for g in range(0, 2 * HEADS, 4):
                    top16(sims, sims2, top_v, top_i, range(g, g + 4))
                    yield
                step(V.tensor_copy(top_f[:], top_i[:]))
                V.tensor_tensor(top_f[:, 0:HEADS, :], top_f[:, 0:HEADS, :],
                                head_off[:].unsqueeze(2).broadcast_to([P, HEADS, TOPK]), ALU.add)
                step(V.tensor_scalar(top_f[:, HEADS:, :], top_f[:, HEADS:, :], float(KEYS), None, ALU.mult))
                pair_up(cand_i, top_f[:, 0:HEADS, :], top_f[:, HEADS:, :])
                step(pair_up(cand_v, top_v[:, 0:HEADS, :], top_v[:, HEADS:, :]))
                yield
                for g in range(0, HEADS, 4):
                    top16(cand_v, cand_v2, fin_v, fin_p, range(g, g + 4))
                    yield
                step(V.tensor_copy(fin_f[:], fin_p[:]))
                for g in range(0, HEADS, 2):
                    place = fin_f[:, g:g + 2, :].rearrange("p g r -> p (g r)")
                    step(V.tensor_tensor(hot[:], place.unsqueeze(2).broadcast_to([P, 2 * TOPK, CAND]),
                                         iota_c[:].unsqueeze(1).broadcast_to([P, 2 * TOPK, CAND]), ALU.is_equal))
                    hot4 = hot[:].rearrange("p (g r) c -> p g r c", g=2)
                    step(V.tensor_tensor(hot4, hot4, cand_i[:, g:g + 2, :].unsqueeze(2)
                                         .broadcast_to([P, 2, TOPK, CAND]), ALU.mult))
                    step(V.tensor_reduce(row_f[:, g * TOPK:(g + 2) * TOPK], hot[:], AX.X, ALU.add))
                    if g < HEADS - 2:
                        yield
                V.tensor_copy(row_i[:, i, :], row_f[:]).then_inc(rows_chosen, 1)
                yield
                step(V.tensor_copy(w_sum[:, 0, :], fin_v[:, :, 0]))
                V.tensor_tensor(fin_v[:], fin_v[:], w_sum[:, 0, :].unsqueeze(2).broadcast_to([P, HEADS, TOPK]),
                                ALU.subtract).then_inc(fin_ready, 1)
                dve.wait_ge(fin_exp, 1)
                dve.sem_inc(fin_exp, -1)
                step(V.tensor_reduce(w_sum[:, 0, :], row_w[:, i, :, :], AX.X, ALU.add))
                step(V.reciprocal(w_sum[:, 1, :], w_sum[:, 0, :]))
                step(V.tensor_tensor(row_w[:, i, :, :], row_w[:, i, :, :],
                                     w_sum[:, 1, :].unsqueeze(2).broadcast_to([P, HEADS, TOPK]), ALU.mult))
                yield

            def gather(b, i):
                for g in range(HEADS):
                    use = (HEADS // RING) * i + g // RING + 1
                    dve.wait_ge(rows_landed[g % RING], b * (PER_USE * (HEADS // RING) * NT) + PER_USE * use)
                    dve.sem_inc(rows_seen, 1)
                    dve.wait_ge(rows_seen, 1)
                    dve.sem_inc(rows_seen, -1)
                    slot = rows[:, g % RING, :, :]
                    step(V.tensor_tensor(slot, slot,
                                         row_w[:, i, g, :].unsqueeze(2).broadcast_to([P, TOPK, 2 * D]), ALU.mult))
                    if g == 0:
                        dve.wait_ge(kv_free, 1)
                        dve.sem_inc(kv_free, -1)
                    step(V.tensor_reduce(kv[:, :, g, :], slot.rearrange("p r (w d) -> p w d r", w=2), AX.X, ALU.add))
                    dve.sem_inc(slot_free[g % RING], 1)
                    if g == HEADS - 1:
                        dve.sem_inc(kv_ready, 1)
                    yield

            def back(b, i):
                hs = h[:, b * NT + i, :]
                yield
                for g in range(HEADS):
                    yield from attend(x, i + 1)
                    V.tensor_scalar(cx[:, g * D:(g + 1) * D], x.O[:, 0:D], x.rinv[:], None, ALU.mult)\
                     .then_inc(x.ctx_read, 1)
                yield
                dve.wait_ge(mem_out_ready, 1)
                dve.sem_inc(mem_out_ready, -1)
                step(V.tensor_tensor(hs, x.O[:, 0:D], hs, ALU.add))
                layer_norm(x, hs)
                yield
                dve.wait_ge(qkv1_ready_dve, 1)
                dve.sem_inc(qkv1_ready_dve, -1)
                V.tensor_tensor(v1[:, i, :], x.O[:, 0:D], bv[:], ALU.add).then_inc(v1_ready, 1)
                yield
                yield from attend(x, i + 1)
                V.tensor_scalar(cx[:, 0:D], x.O[:, 0:D], x.rinv[:], None, ALU.mult).then_inc(x.ctx_read, 1)
                yield
                step(V.tensor_tensor(hs, hs, bproj[:], ALU.add))
                dve.wait_ge(mem_out_ready, 1)
                dve.sem_inc(mem_out_ready, -1)
                step(V.tensor_tensor(hs, x.O[:, 0:D], hs, ALU.add))
                layer_norm(x, hs)
                yield
                dve.wait_ge(logits_ready, 1)
                dve.sem_inc(logits_ready, -1)
                step(V.tensor_tensor(gate[:, 0, :], x.M[:, 0:EXPERTS], gb[:], ALU.add))
                step(V.tensor_reduce(gate_sum[:, 1:2], gate[:, 0, :], AX.X, ALU.max))
                V.tensor_scalar(gate[:, 0, :], gate[:, 0, :], gate_sum[:, 1:2], None, ALU.subtract)\
                 .then_inc(logits_shifted, 1)
                yield
                dve.wait_ge(gate_exp, 1)
                dve.sem_inc(gate_exp, -1)
                step(V.reciprocal(gate_sum[:, 1:2], gate_sum[:, 0:1]))
                step(V.tensor_scalar(gate[:, 2, :], gate[:, 1, :], gate_sum[:, 1:2], None, ALU.mult))
                step(V.max(gate[:, 4, :], gate[:, 2, :]))
                step(V.tensor_copy(gate[:, 5, 0:2], gate[:, 4, 0:2]))
                probs16 = gate[:, 2:4, :].rearrange("p a e -> p (a e)")
                rest16 = gate[:, 6:8, :].rearrange("p a e -> p (a e)")
                step(V.match_replace(rest16, gate[:, 5, :], probs16, 0.0))
                step(V.tensor_tensor(gate[:, 4, :], gate[:, 2, :], gate[:, 6, :], ALU.subtract))
                yield
                dve.wait_ge(experts_ready, 1)
                dve.sem_inc(experts_ready, -1)
                step(V.tensor_tensor(ysc[:], x.O.rearrange("p (e d) -> p e d", d=D), b2_s[:], ALU.add))
                dve.sem_inc(experts_read, 1)
                step(V.tensor_tensor(ysc[:], ysc[:], gate[:, 4, :].unsqueeze(2).broadcast_to([P, EXPERTS, D]),
                                     ALU.mult))
                step(V.tensor_reduce(ysum[:], ysc[:].rearrange("p e d -> p d e"), AX.X, ALU.add))
                dve.wait_ge(out_stored, 16)
                dve.sem_inc(out_stored, -16)
                V.tensor_tensor(outt[:], hs, ysum[:], ALU.add).then_inc(out_ready, 1)
                yield

            dve.wait_ge(masks_ready_dve, 1)
            dve.sem_inc(masks_ready_dve, -1)
            dve.wait_ge(ids_loaded, 16)
            step(V.tensor_copy(ids_f[:, 0, :], ids_s[:]))
            step(V.tensor_scalar(ids_f[:, 1, :], ids_f[:, 0, :], 0.0, float(VOCAB), ALU.is_lt, ALU.mult))
            step(V.tensor_tensor(ids_f[:, 0, :], ids_f[:, 0, :], ids_f[:, 1, :], ALU.add))
            step(V.tensor_scalar(ids_f[:, 0, :], ids_f[:, 0, :], 0.0, float(VOCAB - 1), ALU.max, ALU.min))
            V.tensor_scalar(ids_u[:], ids_f[:, 0, :], float(PLE_GROUPS), float(PLE_LAYER),
                            ALU.mult, ALU.add).then_inc(text_ids_ready, 1)
            step(V.memset(gate[:, 2:8, :], -1.0))
            dve.wait_ge(w_loaded_dve, 1)
            dve.sem_inc(w_loaded_dve, -1)
            step(V.tensor_tensor(posb[:], posb[:], tokb[:].unsqueeze(1).broadcast_to([P, PT_TILES, D]), ALU.add))
            for g in range(RING):
                dve.sem_inc(slot_free[g], 1)
            dve.sem_inc(out_stored, 16)
            for free in (x.xn_free, y.xn_free, kv_free):
                dve.sem_inc(free, 1)
            dve.wait_ge(text_loaded, 16 * BATCH)
            for _ in front(0):
                pass
            for i in range(LEAD):
                for _ in select(0, i):
                    pass
            for _ in gather(0, 0):
                pass
            with dve.Fori(0, BATCH - 1) as b:
                for i in range(NT):
                    if i + LEAD < NT:
                        run((back(b, i), gather(b, i + 1), select(b, i + LEAD)), (BACK, HEADS, SELECT))
                    elif i + LEAD == NT:
                        run((back(b, i), gather(b, i + 1), chain_of(front(b + 1), select(b + 1, 0))),
                            (BACK, HEADS, FRONT + SELECT))
                    elif i + 1 < NT:
                        run((back(b, i), gather(b, i + 1), select(b + 1, i + LEAD - NT)), (BACK, HEADS, SELECT))
                    else:
                        run((back(b, i), gather(b + 1, 0), select(b + 1, i + LEAD - NT)), (BACK, HEADS, SELECT))
            b = BATCH - 1
            for i in range(NT):
                if i + LEAD < NT:
                    run((back(b, i), gather(b, i + 1), select(b, i + LEAD)), (BACK, HEADS, SELECT))
                elif i < NT - 1:
                    run((back(b, i), gather(b, i + 1)), (BACK, HEADS))
                else:
                    run((back(b, i),), (BACK,))


def kernel(**inputs):
    import numpy as np
    import concourse.bacc as bacc
    from concourse.bass_utils import run_bass_kernel_spmd

    a = {k: np.asarray(v) for k, v in inputs.items()}
    arrays = {
        "x_in": a["x"], "ids": a["x_txt"].T,
        "tok_wT": a["L0_tok_W"].T, "tok_b": a["L0_tok_b"], "pos": a["L0_tok_pos_embed"][0],
        "ple": a["L0_txt_ple_table"].reshape(VOCAB * PLE_GROUPS, D),
        "wqT": a["L0_attn_Wq"].T, "wkT": a["L0_attn_Wk"].T, "wvT": a["L0_attn_Wv"].T,
        "wq_pk": a["L0_ffn_Wq_pk"], "keysT": a["L0_ffn_pk_keys"].transpose(0, 2, 3, 1),
        "wq_mem": a["L0_ffn_Wq"],
        "kv_table": np.concatenate([a["L0_ffn_keys_table"], a["L0_ffn_values_table"]], axis=1),
        "wo": a["L0_ffn_Wo"], "w_qkv": a["L1_attn_W_qkv"], "b_qkv": a["L1_attn_b_qkv"],
        "w_proj": a["L1_attn_W_proj"], "b_proj": a["L1_attn_b_proj"],
        "gate_w": a["L1_ffn_gate_w"], "gate_b": a["L1_ffn_gate_b"],
        "w1": a["L1_ffn_W1"], "b1T": a["L1_ffn_b1"].T, "w2": a["L1_ffn_W2"], "b2": a["L1_ffn_b2"],
    }
    arrays = {k: np.ascontiguousarray(v) for k, v in arrays.items()}
    nc = bacc.Bacc("TRN2", target_bir_lowering=False, num_devices=1)
    args = {k: nc.dram_tensor(k, v.shape, mybir.dt.from_np(v.dtype), kind="ExternalInput").ap()
            for k, v in arrays.items()}
    out = nc.dram_tensor("out", (BATCH, TOKENS, D), F32, kind="ExternalOutput").ap()
    build(nc, out=out, **args)
    result = run_bass_kernel_spmd(nc, [arrays], core_ids=[0])
    return result.results[0]["out"]
```

```python
from contextlib import ExitStack

import concourse.bass as bass
from concourse import mybir

F32 = mybir.dt.float32
BF16 = mybir.dt.bfloat16
I32 = mybir.dt.int32
U32 = mybir.dt.uint32
U16 = mybir.dt.uint16
ALU = mybir.AluOpType
ACT = mybir.ActivationFunctionType
AX = mybir.AxisListType

P = 128
BATCH, MELS, FRAMES, PATCH = 4, 128, 512, 8
D = 64
PATCHES = (MELS // PATCH) * (FRAMES // PATCH)
TEXT = 128
TOKENS = PATCHES + TEXT
NT = TOKENS // P
PT_TILES = PATCHES // P
FJ = FRAMES // PATCH
VOCAB, PLE_GROUPS, PLE_LAYER = 32000, 8, 3
HEADS, KEYS, DK, TOPK = 8, 64, 32, 16
SLOTS = KEYS * KEYS
RING = 4
EXPERTS, HID = 8, 128
EPS = 1e-5
BANK = 512
LOWEST = -3.4028234663852886e38
MASKED = -1e30
PER_USE = 16 * TOPK
RSQRT_SEED = float(0x5F3759DF)
LEAD = 3
GROUPS = 4
TOP_STAGES, FINAL_STAGES, MAP_STAGES = 2 * HEADS // GROUPS, HEADS // GROUPS, 3 * HEADS // GROUPS
SELECT = [4, 2.5, 7, 4, 7] + TOP_STAGES * [3] + [4] + FINAL_STAGES * [3] + MAP_STAGES * [2.2] + [3, 2]
SELECT_PSUM = 6
GATHER = (2 * HEADS + 1) * [1]
FRONT = [4, 5, 4]


def heads_stages(n):
    return [6, 3] + HEADS * [5 + 1.6 * n] + [4, 3]


def tail_stages(n):
    return [4, 5, 3, 4, 4 + 0.8 * n, 4, 5, 7, 3, 7, 4, 1]


def depth(n):
    return 2 if n * P <= 2 * BANK else 1


FRONT_STEPS = NT - LEAD - 1
FRONT_TILES = {s: range(-(-NT * (s - 1) // FRONT_STEPS), -(-NT * s // FRONT_STEPS)) for s in range(1, FRONT_STEPS + 1)}
ROWS = [(a, TOPK // (a + 1)) for a in range(TOPK)]
CAND = sum(n for _, n in ROWS)
BLOCKS = []
_col = 0
for _a, _n in ROWS:
    if BLOCKS and BLOCKS[-1][2] == _n:
        BLOCKS[-1][1] += 1
    else:
        BLOCKS.append([_a, 1, _n, _col])
    _col += _n


def order(chains):
    spots = []
    for n, (_, start, times) in enumerate(chains):
        spots += [(start + (1 - start) * (sum(times[:k]) + times[k] / 2) / sum(times), n) for k in range(len(times))]
    return [n for _, n in sorted(spots)]


def run(*chains):
    for n in order(chains):
        if chains[n][0] is not None:
            next(chains[n][0])
    for c, _, _ in chains:
        assert c is None or next(c, None) is None


def chain_of(*chains):
    for c in chains:
        yield from c


def all_steps(engine, loaded, front, select, gather, heads, tail):
    freed = sum(SELECT[:SELECT_PSUM]) / sum(SELECT)

    def step(b, s, last=False):
        def at(chain, k):
            return chain(b + 1, k - NT) if k >= NT else chain(b, k)

        def there(k):
            return not last or k < NT

        chains = []
        if there(s):
            chains.append((at(heads, s), 0, heads_stages(s % NT + 1)))
        if there(s + 1):
            chains.append((at(gather, s + 1), 0, GATHER))
        if there(s + LEAD):
            chains.append((at(select, s + LEAD), 0, SELECT))
        late, times = [], []
        if not last and s in FRONT_TILES:
            late += [front(b + 1, i) for i in FRONT_TILES[s]]
            times += FRONT * len(late)
        if s > 0:
            late.append(tail(b, s - 1))
            times += tail_stages(s)
        if late:
            chains.append((chain_of(*late), freed if there(s + LEAD) else 0, times))
        run(*chains)

    tiles = [front(0, i) for i in range(NT)]
    next(tiles[0])
    for i in range(NT):
        next(tiles[i])
        if i + 1 < NT:
            next(tiles[i + 1])
        next(tiles[i])
    loaded()
    run((select(0, 0), 0, SELECT))
    run((gather(0, 0), 0, GATHER), (chain_of(select(0, 1), select(0, 2)), 0, SELECT + SELECT))
    run((heads(0, 0), 0, heads_stages(1)), (gather(0, 1), 0, GATHER), (select(0, LEAD), 0, SELECT))
    with engine.Fori(0, BATCH - 1) as b:
        for s in range(1, NT + 1):
            step(b, s)
    for s in range(1, NT + 1):
        step(BATCH - 1, s, last=True)


def probsT_spot(sets, o, j):
    return o + j * P if sets == 2 else 3 * BANK + j % 8 * P


class Scratch:
    pass


def build(nc, x_in, ids, tok_wT, tok_b, pos, ple, wqT, wkT, wvT, wq_pk, keysT, wq_mem, kv_table, wo,
          w_qkv, b_qkv, w_proj, b_proj, gate_w, gate_b, w1, b1T, w2, b2, out):
    ctx = ExitStack()
    with ctx:
        def sb(name, shape, dt=F32):
            return ctx.enter_context(nc.sbuf_tensor(name, shape, dt))

        def ps(name, shape, dt=F32):
            return ctx.enter_context(nc.psum_tensor(name, shape, dt))

        def sem(name):
            return ctx.enter_context(nc.semaphore(name))

        ident = sb("ident", [P, P])
        ident_h = sb("ident_h", [P, P], BF16)
        causal = sb("causal", [P, P], BF16)
        places = sb("places", [P, CAND, GROUPS], U16)
        head_off = sb("head_off", [P, HEADS])
        tokw = sb("tokw", [D, D])
        posb = sb("posb", [P, PT_TILES, D])
        tokb = sb("tokb", [P, D])
        w0 = sb("w0", [D, 3, D])
        wpk = sb("wpk", [D, 2 * HEADS * DK])
        keys_bd = sb("keys_bd", [P, 4, 4 * KEYS])
        wqm = sb("wqm", [D, HEADS * D])
        wo_s = sb("wo_s", [P, 4, D])
        wqkv = sb("wqkv", [D, 3 * D])
        bq = sb("bq", [D, 2])
        bq8 = sb("bq8", [D, 1])
        bv = sb("bv", [P, D])
        wproj = sb("wproj", [D, D])
        bproj = sb("bproj", [P, D])
        gw = sb("gw", [D, EXPERTS])
        gb = sb("gb", [P, EXPERTS])
        w1_s = sb("w1_s", [D, EXPERTS, HID])
        b1_s = sb("b1_s", [HID, EXPERTS])
        w2_s = sb("w2_s", [HID, EXPERTS, D])
        b2_s = sb("b2_s", [P, EXPERTS, D])
        ids_s = sb("ids_s", [P, BATCH], I32)
        ids_f = sb("ids_f", [P, 2, BATCH])
        ids_u = sb("ids_u", [P, BATCH], U32)
        text = sb("text", [P, BATCH, D])

        h = sb("h", [P, BATCH * NT, D])
        patch = sb("patch", [P, PT_TILES, D])
        patchT = sb("patchT", [D, P])
        qk0 = sb("qk0", [D, 2, TOKENS])
        v0 = sb("v0", [P, NT, D])
        next_qk0 = sb("next_qk0", [D, 2, TOKENS])
        next_v0 = sb("next_v0", [P, NT, D])
        xn2T = sb("xn2T", [D, NT, P])
        qpkT = sb("qpkT", [P, BANK])
        sims = sb("sims", [P, 2 * HEADS, KEYS])
        top_v = sb("top_v", [P, 2 * HEADS, TOPK])
        top_i = sb("top_i", [P, 2 * HEADS, TOPK], U16)
        cand_v = sb("cand_v", [P, HEADS, CAND])
        cand_v2 = sb("cand_v2", [P, HEADS, CAND])
        cand_i = sb("cand_i", [P, CAND, HEADS], U16)
        fin_v = sb("fin_v", [P, HEADS, TOPK])
        fin_p = sb("fin_p", [P, HEADS, TOPK], U16)
        fin_t = sb("fin_t", [P, TOPK, GROUPS], U16)
        hot = sb("hot", [P, CAND, TOPK * GROUPS], U16)
        sims2 = hot[:].rearrange("p c k -> p (c k)").bitcast(F32)[:, 0:2 * HEADS * KEYS].rearrange(
            "p (g k) -> p g k", k=KEYS)
        row_f = sb("row_f", [P, TOPK * GROUPS])
        w_sum = sb("w_sum", [P, 2, HEADS])
        row_i = sb("row_i", [P, NT, HEADS // GROUPS, TOPK, GROUPS], U32)
        row_w = sb("row_w", [P, NT, HEADS, TOPK])
        rows = sb("rows", [P, RING, TOPK, 2 * D])
        kv = sb("kv", [P, 2, HEADS, D])
        kT = sb("kT", [P, 4, TOKENS])
        vm = sb("vm", [P, NT, HEADS * D])
        qmT = sb("qmT", [P, BANK])
        cx = sb("cx", [P, BANK])
        cxT = sb("cxT", [P, BANK])
        ctx1 = sb("ctx1", [P, D])
        ctx1T = sb("ctx1T", [D, P])
        q1T = sb("q1T", [D, P])
        k1T = sb("k1T", [D, TOKENS])
        v1 = sb("v1", [P, NT, D])
        gate = sb("gate", [P, 8, EXPERTS])
        gate_sum = sb("gate_sum", [P, 2])
        gelT = sb("gelT", [HID, EXPERTS, P])
        ysc = sb("ysc", [P, EXPERTS, D])
        ysum = sb("ysum", [P, D])
        outt = sb("outt", [P, D])

        def scratch(n, banks, narrow):
            t = Scratch()
            t.ps = ps(f"{n}_ps", [P, banks * BANK])
            t.O = t.ps[:, 0:BANK]
            t.M = t.ps[:, narrow:banks * BANK]
            t.probs = sb(f"{n}_probs", [P, TOKENS])
            t.probsT = sb(f"{n}_probsT", [P, TOKENS])
            t.nmax = sb(f"{n}_nmax", [P, 2])
            t.rsum = sb(f"{n}_rsum", [P, 2])
            t.rinv = sb(f"{n}_rinv", [P, 1])
            t.scores_ready = sem(f"{n}_scores_ready")
            t.negmax_ready = sem(f"{n}_negmax_ready")
            t.probs_ready = sem(f"{n}_probs_ready")
            t.probsT_ready = sem(f"{n}_probsT_ready")
            t.probsT_copied = sem(f"{n}_probsT_copied")
            t.ctx_ready = sem(f"{n}_ctx_ready")
            t.ctx_read = sem(f"{n}_ctx_read")
            return t

        x = scratch("heads", 5, 4 * BANK)
        y = scratch("select", 3, NT * P)
        y.st6 = sb("st6", [P, 6])
        y.mv = sb("mv", [P, 2])
        y.rs = sb("rs", [P, 8])
        y.rsi = sb("rsi", [P, 2], I32)
        y.xn = sb("xn", [P, D])
        y.xnT = sb("xnT", [D, P])
        y.xn_ready = sem("xn_ready")
        y.xn_free = sem("xn_free")
        y.xnT_ready = sem("xnT_ready")
        y.xnT_copied = sem("xnT_copied")

        front_loaded = sem("front_loaded")
        const_loaded = sem("const_loaded")
        w_loaded_pe = sem("w_loaded_pe")
        w_loaded_act = sem("w_loaded_act")
        w_loaded_dve = sem("w_loaded_dve")
        keys_zeroed = sem("keys_zeroed")
        keys_loaded = sem("keys_loaded")
        ids_loaded = sem("ids_loaded")
        pool_step = sem("pool_step")
        masks_ready = sem("masks_ready")
        masks_ready_dve = sem("masks_ready_dve")
        text_ids_ready = sem("text_ids_ready")
        text_loaded = sem("text_loaded")
        bq8_ready = sem("bq8_ready")
        patch_loaded = sem("patch_loaded")
        patch_free = sem("patch_free")
        dve_step = sem("dve_step")
        patchT_ready = sem("patchT_ready")
        patchT_copied = sem("patchT_copied")
        emb_ready = sem("emb_ready")
        emb_read = sem("emb_read")
        qkv0_ready = sem("qkv0_ready")
        qkv0_copied = sem("qkv0_copied")
        qkv0_complete = sem("qkv0_complete")
        qkv0_moved = sem("qkv0_moved")
        qpk_ready = sem("qpk_ready")
        qpk_copied = sem("qpk_copied")
        sims_ready = sem("sims_ready")
        sims_copied = sem("sims_copied")
        sims_seen = sem("sims_seen")
        fin_ready = sem("fin_ready")
        fin_exp = sem("fin_exp")
        weights_ready = sem("weights_ready")
        rows_chosen = sem("rows_chosen")
        rows_landed = [sem(f"rows_landed{n}") for n in range(RING)]
        rows_seen = sem("rows_seen")
        rows_scaled = sem("rows_scaled")
        slot_free = [sem(f"slot_free{n}") for n in range(RING)]
        kv_ready = sem("kv_ready")
        kv_free = sem("kv_free")
        kq_ready = sem("kq_ready")
        kq_copied = sem("kq_copied")
        heads_ready = sem("heads_ready")
        headsT_ready = sem("headsT_ready")
        headsT_copied = sem("headsT_copied")
        mem_out_ready = sem("mem_out_ready")
        mem_out_read = sem("mem_out_read")
        ctx1T_ready = sem("ctx1T_ready")
        ctx1T_copied = sem("ctx1T_copied")
        proj_ready = sem("proj_ready")
        qkv1_ready = sem("qkv1_ready")
        qkv1_ready_dve = sem("qkv1_ready_dve")
        qk1_copied = sem("qk1_copied")
        v1_ready = sem("v1_ready")
        logits_ready = sem("logits_ready")
        logits_shifted = sem("logits_shifted")
        gate_exp = sem("gate_exp")
        hidden_ready = sem("hidden_ready")
        gelu_ready = sem("gelu_ready")
        experts_ready = sem("experts_ready")
        experts_read = sem("experts_read")
        out_ready = sem("out_ready")
        out_stored = sem("out_stored")

        block = ctx.enter_context(nc.Block())

        @block.sync
        def _(sp):
            sp.dma_start(ids_s[:], ids).then_inc(ids_loaded, 16)

            def load_patches(b):
                for m in range(MELS // PATCH):
                    src = x_in[b, 0, m * PATCH:(m + 1) * PATCH, :].rearrange("p (j f) -> j p f", f=PATCH)
                    dst = patch[FJ * (m % 2):FJ * (m % 2) + FJ, m // 2, :].rearrange("j (p f) -> j p f", f=PATCH)
                    sp.dma_start(dst, src).then_inc(patch_loaded, 16)

            first = [
                (tokw[:], tok_wT), (posb[:], pos.rearrange("(t p) e -> p t e", p=P)),
                (tokb[:], tok_b.partition_broadcast(P)),
                (w0[:, 0, :], wqT), (w0[:, 1, :], wkT), (w0[:, 2, :], wvT),
            ]
            for dst, src in first:
                sp.dma_start(dst, src).then_inc(front_loaded, 16)
            load_patches(0)
            sp.wait_ge(front_loaded, 16 * len(first))
            for s in (w_loaded_pe, w_loaded_dve):
                sp.sem_inc(s, 1)
            loads = [
                (wpk[:], wq_pk), (wqm[:], wq_mem), (wo_s[:], wo.rearrange("(c p) e -> p c e", p=P)),
                (wqkv[:], w_qkv), (bq[:, 0:1], b_qkv[0:D].unsqueeze(1)), (bq[:, 1:2], b_qkv[D:2 * D].unsqueeze(1)),
                (bv[:], b_qkv[2 * D:3 * D].partition_broadcast(P)),
                (wproj[:], w_proj), (bproj[:], b_proj.partition_broadcast(P)),
                (gw[:], gate_w), (gb[:], gate_b.partition_broadcast(P)),
                (w1_s[:], w1.rearrange("e d k -> d e k")),
                (b1_s[:], b1T), (w2_s[:], w2.rearrange("e k d -> k e d")),
                (b2_s[:].rearrange("p e d -> p (e d)"), b2.rearrange("e d -> (e d)").partition_broadcast(P)),
            ]
            for dst, src in loads:
                sp.dma_start(dst, src).then_inc(const_loaded, 16)
            sp.wait_ge(const_loaded, 16 * len(loads))
            for s in (w_loaded_pe, w_loaded_act, w_loaded_dve):
                sp.sem_inc(s, 1)
            sp.wait_ge(keys_zeroed, 1)
            for p in range(2):
                for g in range(HEADS):
                    r = DK * (g % 4)
                    sp.dma_start(keys_bd[r:r + DK, 2 * p + g // 4, KEYS * (g % 4):KEYS * (g % 4) + KEYS],
                                 keysT[p, g]).then_inc(keys_loaded, 16)
            for b in range(1, BATCH):
                sp.wait_ge(patch_free, 1)
                sp.sem_inc(patch_free, -1)
                load_patches(b)

        @block.gpsimd
        def _(pool):
            def step(ins):
                ins.then_inc(pool_step, 1)
                pool.wait_ge(pool_step, 1)
                pool.sem_inc(pool_step, -1)

            pool.memset(keys_bd[:], 0.0).then_inc(keys_zeroed, 1)
            step(pool.memset(ident[:], 0.0))
            step(pool.affine_select(out=ident[:], in_=ident[:], compare_op=ALU.not_equal, fill=1.0, base=0,
                                    pattern=[[-1, P]], channel_multiplier=1))
            step(pool.tensor_copy(ident_h[:], ident[:]))
            step(pool.memset(causal[:], 0.0))
            step(pool.affine_select(out=causal[:], in_=causal[:], compare_op=ALU.is_ge, fill=MASKED, base=0,
                                    pattern=[[-1, P]], channel_multiplier=1))
            step(pool.iota(cand_v[:, 0, :], pattern=[[1, CAND]], base=0, channel_multiplier=0,
                           allow_small_or_imprecise_dtypes=True))
            step(pool.iota(head_off[:], pattern=[[SLOTS, HEADS]], base=0, channel_multiplier=0,
                           allow_small_or_imprecise_dtypes=True))
            pool.sem_inc(masks_ready, 1)
            pool.sem_inc(masks_ready_dve, 1)
            pool.wait_ge(text_ids_ready, 1)
            pool.sem_inc(text_ids_ready, -1)
            for b in range(BATCH):
                pool.indirect_dma_start(
                    out=text[:, b, :], out_offset=None, in_=ple,
                    in_offset=bass.IndirectOffsetOnAxis(ap=ids_u[:, b:b + 1], axis=0)).then_inc(text_loaded, 16)

            with pool.Fori(0, BATCH) as _b:
                for i in range(NT):
                    for g in range(HEADS):
                        if g % GROUPS == 0:
                            pool.wait_ge(rows_chosen, 1)
                            pool.sem_inc(rows_chosen, -1)
                        pool.wait_ge(slot_free[g % RING], 1)
                        pool.sem_inc(slot_free[g % RING], -1)
                        for r in range(TOPK):
                            pool.indirect_dma_start(
                                out=rows[:, g % RING, r, :], out_offset=None, in_=kv_table,
                                in_offset=bass.IndirectOffsetOnAxis(
                                    ap=row_i[:, i, g // GROUPS, r, g % GROUPS:g % GROUPS + 1], axis=0),
                            ).then_inc(rows_landed[g % RING], 16)

        @block.tensor
        def _(pe):
            mm = nc.tensor.matmul

            def transpose_xn():
                pe.wait_ge(y.xn_ready, 1)
                pe.sem_inc(y.xn_ready, -1)
                nc.tensor.transpose(y.M[0:D, 0:P], y.xn[:], ident[:]).then_inc(y.xnT_ready, 1)
                pe.wait_ge(y.xnT_copied, 1)
                pe.sem_inc(y.xnT_copied, -1)
                pe.sem_inc(y.xn_free, 1)

            def scores(t, q, k, n, masked, o=0):
                for c in range(0, n * P, BANK):
                    e = min(c + BANK, n * P)
                    diag = masked and e == n * P
                    last = mm(t.ps[:, o + c:o + e], q, k[:, c:e], start=True, stop=not diag)
                    if diag:
                        last = mm(t.ps[:, o + e - P:o + e], ident_h[:], causal[:], start=False, stop=True)
                last.then_inc(t.scores_ready, 1)

            def context(t, v, n, o=0, first=True):
                groups = range(0, n, 4)
                pe.wait_ge(t.probs_ready, 1)
                pe.sem_inc(t.probs_ready, -1)
                for j0 in groups:
                    for j in range(j0, min(j0 + 4, n)):
                        last = nc.tensor.transpose(t.ps[:, o + j * P:o + (j + 1) * P],
                                                   t.probs[:, j * P:(j + 1) * P], ident[:])
                    last.then_inc(t.probsT_ready, 1)
                if not first:
                    pe.wait_ge(t.ctx_read, 1)
                    pe.sem_inc(t.ctx_read, -1)
                if t is y:
                    pe.wait_ge(t.probsT_copied, len(groups))
                    pe.sem_inc(t.probsT_copied, -(len(groups)))
                for j0 in groups:
                    if t is x:
                        pe.wait_ge(t.probsT_copied, 1)
                        pe.sem_inc(t.probsT_copied, -1)
                    for j in range(j0, min(j0 + 4, n)):
                        last = mm(t.M[:, 0:D], t.probsT[:, j * P:(j + 1) * P], v(j), start=(j == 0), stop=(j == n - 1))
                last.then_inc(t.ctx_ready, 1)

            def front(_b, i):
                if i < PT_TILES:
                    if i == 0:
                        pe.wait_ge(patch_loaded, 16 * (MELS // PATCH))
                        pe.sem_inc(patch_loaded, -(16 * (MELS // PATCH)))
                    nc.tensor.transpose(y.ps[0:D, BANK:BANK + P], patch[:, i, :], ident[:]).then_inc(patchT_ready, 1)
                    pe.wait_ge(patchT_copied, 1)
                    pe.sem_inc(patchT_copied, -1)
                    mm(y.O[:, 0:D], patchT[:], tokw[:], start=True, stop=True).then_inc(emb_ready, 1)
                    if i == PT_TILES - 1:
                        pe.sem_inc(patch_free, 1)
                yield
                if i < PT_TILES:
                    pe.wait_ge(emb_read, 1)
                    pe.sem_inc(emb_read, -1)
                yield
                transpose_xn()
                mm(y.M[0:D, 0:P], w0[:, 0, :], y.xnT[:], start=True, stop=True)
                mm(y.M[0:D, P:2 * P], w0[:, 1, :], y.xnT[:], start=True, stop=True)
                mm(y.M[:, 2 * P:2 * P + D], y.xnT[:], w0[:, 2, :], start=True, stop=True).then_inc(qkv0_ready, 1)
                pe.wait_ge(qkv0_copied, 1)
                pe.sem_inc(qkv0_copied, -1)
                if i == NT - 1:
                    pe.sem_inc(qkv0_complete, 1)
                yield

            def select(_b, i):
                if i == 0:
                    pe.wait_ge(qkv0_moved, 1)
                    pe.sem_inc(qkv0_moved, -1)
                scores(y, qk0[:, 0, i * P:(i + 1) * P], qk0[:, 1, :], NT, False)
                yield
                yield
                context(y, lambda j: v0[:, j, :], NT)
                yield
                yield
                transpose_xn()
                for c in range(4):
                    last = mm(y.O[:, c * P:(c + 1) * P], wpk[:, c * P:(c + 1) * P], xn2T[:, i, :], start=True, stop=True)
                last.then_inc(qpk_ready, 1)
                pe.wait_ge(qpk_copied, 1)
                pe.sem_inc(qpk_copied, -1)
                for c in range(4):
                    last = mm(y.ps[:, c * 256:(c + 1) * 256], qpkT[:, c * P:(c + 1) * P], keys_bd[:, c, :],
                              start=True, stop=True)
                last.then_inc(sims_ready, 1)
                yield
                pe.wait_ge(sims_seen, 1)
                pe.sem_inc(sims_seen, -1)
                yield
                for _ in SELECT[SELECT_PSUM:]:
                    yield

            def heads(_b, i):
                pe.wait_ge(kv_ready, 1)
                pe.sem_inc(kv_ready, -1)
                for c in range(4):
                    nc.tensor.transpose(x.O[:, c * P:(c + 1) * P], kv[:, 0, 2 * c:2 * c + 2, :].rearrange(
                        "p g d -> p (g d)"), ident[:])
                for c in range(4):
                    last = mm(x.M[:, c * P:(c + 1) * P], wqm[:, c * P:(c + 1) * P], xn2T[:, i, :], start=True, stop=True)
                last.then_inc(kq_ready, 1)
                pe.wait_ge(kq_copied, 1)
                pe.sem_inc(kq_copied, -1)

                sets = depth(i + 1)

                def head_scores(g):
                    r = D * (g % 2)
                    scores(x, qmT[r:r + D, (g // 2) * P:(g // 2 + 1) * P], kT[r:r + D, g // 2, :], i + 1, True,
                           g % sets * 2 * BANK)

                for g in range(sets):
                    head_scores(g)
                yield
                yield
                for g in range(HEADS if sets == 1 else 0):
                    pe.wait_ge(x.probs_ready, 1)
                    pe.sem_inc(x.probs_ready, -1)
                    if g + 1 < HEADS:
                        head_scores(g + 1)
                    for j0 in (0, 4, 8):
                        if j0 == 4 and g > 0:
                            pe.wait_ge(x.ctx_read, 1)
                            pe.sem_inc(x.ctx_read, -1)
                        if j0 == 8:
                            pe.wait_ge(x.probsT_copied, 1)
                            pe.sem_inc(x.probsT_copied, -1)
                        for j in range(j0, min(j0 + 4, NT)):
                            o = probsT_spot(1, 0, j)
                            last = nc.tensor.transpose(x.ps[:, o:o + P], x.probs[:, j * P:(j + 1) * P], ident[:])
                        last.then_inc(x.probsT_ready, 1)
                    pe.wait_ge(x.probsT_copied, 2)
                    pe.sem_inc(x.probsT_copied, -2)
                    for j in range(NT):
                        last = mm(x.M[:, 0:D], x.probsT[:, j * P:(j + 1) * P], vm[:, j, g * D:(g + 1) * D],
                                  start=(j == 0), stop=(j == NT - 1))
                    last.then_inc(x.ctx_ready, 1)
                    yield
                for g in range(HEADS if sets == 2 else 0):
                    context(x, lambda j: vm[:, j, g * D:(g + 1) * D], i + 1, g % sets * 2 * BANK, first=(g == 0))
                    if g + sets < HEADS:
                        head_scores(g + sets)
                    yield
                pe.wait_ge(x.ctx_read, 1)
                pe.sem_inc(x.ctx_read, -1)
                for c in range(4):
                    last = nc.tensor.transpose(x.M[:, c * P:(c + 1) * P], cx[:, c * P:(c + 1) * P], ident[:])
                last.then_inc(headsT_ready, 1)
                pe.wait_ge(headsT_copied, 1)
                pe.sem_inc(headsT_copied, -1)
                for c in range(4):
                    last = mm(x.O[:, 0:D], cxT[:, c * P:(c + 1) * P], wo_s[:, c, :], start=(c == 0), stop=(c == 3))
                last.then_inc(mem_out_ready, 1)
                yield
                pe.wait_ge(mem_out_read, 1)
                pe.sem_inc(mem_out_read, -1)
                yield

            def tail(_b, i):
                yield
                transpose_xn()
                mm(y.M[0:D, 0:P], wqkv[:, 0:D], y.xnT[:], start=True, stop=True)
                mm(y.M[0:D, P:2 * P], wqkv[:, D:2 * D], y.xnT[:], start=True, stop=True).then_inc(qkv1_ready, 1)
                mm(y.O[:, 0:D], y.xnT[:], wqkv[:, 2 * D:3 * D], start=True, stop=True).then_inc(qkv1_ready_dve, 1)
                pe.wait_ge(qk1_copied, 1)
                pe.sem_inc(qk1_copied, -1)
                yield
                pe.wait_ge(v1_ready, 1)
                pe.sem_inc(v1_ready, -1)
                scores(y, q1T[:], k1T[:], i + 1, True)
                yield
                yield
                context(y, lambda j: v1[:, j, :], i + 1)
                yield
                pe.wait_ge(y.ctx_read, 1)
                pe.sem_inc(y.ctx_read, -1)
                nc.tensor.transpose(y.M[0:D, 0:P], ctx1[:], ident[:]).then_inc(ctx1T_ready, 1)
                pe.wait_ge(ctx1T_copied, 1)
                pe.sem_inc(ctx1T_copied, -1)
                mm(y.O[:, 0:D], ctx1T[:], wproj[:], start=True, stop=True).then_inc(proj_ready, 1)
                yield
                yield
                transpose_xn()
                mm(y.M[:, 0:EXPERTS], y.xnT[:], gw[:], start=True, stop=True).then_inc(logits_ready, 1)
                for e in range(EXPERTS):
                    last = mm(y.ps[:, e * P:(e + 1) * P], w1_s[:, e, :], y.xnT[:], start=True, stop=True)
                last.then_inc(hidden_ready, 1)
                yield
                yield
                yield
                pe.wait_ge(gelu_ready, 1)
                pe.sem_inc(gelu_ready, -1)
                for e in range(EXPERTS):
                    last = mm(y.O[:, e * D:(e + 1) * D], gelT[:, e, :], w2_s[:, e, :], start=True, stop=True)
                last.then_inc(experts_ready, 1)
                yield
                pe.wait_ge(experts_read, 1)
                pe.sem_inc(experts_read, -1)
                yield

            pe.wait_ge(masks_ready, 1)
            pe.sem_inc(masks_ready, -1)
            pe.wait_ge(w_loaded_pe, 1)
            pe.sem_inc(w_loaded_pe, -1)
            def loaded():
                pe.wait_ge(w_loaded_pe, 1)
                pe.sem_inc(w_loaded_pe, -1)
                pe.wait_ge(keys_loaded, 16 * 2 * HEADS)

            all_steps(pe, loaded, front, select, lambda _b, _i: None, heads, tail)

        @block.scalar
        def _(act):
            def copy(dst, src, done, scale=1.0):
                nc.scalar.activation(dst, src, ACT.Copy, scale=scale).then_inc(done, 1)

            def copy_xnT(dst):
                act.wait_ge(y.xnT_ready, 1)
                act.sem_inc(y.xnT_ready, -1)
                copy(dst, y.M[0:D, 0:P], y.xnT_copied)

            def exponential(t, n, g=0, o=0):
                act.wait_ge(t.negmax_ready, 1)
                act.sem_inc(t.negmax_ready, -1)
                nc.scalar.activation(t.probs[:, 0:n * P], t.ps[:, o:o + n * P], ACT.Exp, bias=t.nmax[:, g % 2:g % 2 + 1],
                                     accum_out=t.rsum[:, g % 2:g % 2 + 1]).then_inc(t.probs_ready, 1)

            def copy_probsT(t, n, o=0, sets=2):
                for j in range(0, n, 4):
                    act.wait_ge(t.probsT_ready, 1)
                    act.sem_inc(t.probsT_ready, -1)
                    c, m, spot = j * P, min(4, n - j) * P, probsT_spot(sets, o, j)
                    copy(t.probsT[:, c:c + m], t.ps[:, spot:spot + m], t.probsT_copied)

            def front(_b, i):
                if i < PT_TILES:
                    act.wait_ge(patchT_ready, 1)
                    act.sem_inc(patchT_ready, -1)
                    copy(patchT[:], y.ps[0:D, BANK:BANK + P], patchT_copied)
                yield
                yield
                copy_xnT(y.xnT[:])
                act.wait_ge(qkv0_ready, 1)
                act.sem_inc(qkv0_ready, -1)
                nc.scalar.activation(next_qk0[:, :, i * P:(i + 1) * P],
                                     y.M[0:D, 0:2 * P].rearrange("d (w t) -> d w t", w=2), ACT.Copy)
                copy(next_v0[:, i, :], y.M[:, 2 * P:2 * P + D], qkv0_copied)
                yield

            def select(_b, i):
                if i == 0:
                    act.wait_ge(qkv0_complete, 1)
                    act.sem_inc(qkv0_complete, -1)
                    nc.scalar.activation(qk0[:], next_qk0[:], ACT.Copy)
                    copy(v0[:], next_v0[:], qkv0_moved)
                yield
                yield
                exponential(y, NT)
                copy_probsT(y, NT)
                yield
                yield
                copy_xnT(xn2T[:, i, :])
                act.wait_ge(qpk_ready, 1)
                act.sem_inc(qpk_ready, -1)
                copy(qpkT[:], y.O, qpk_copied)
                act.wait_ge(sims_ready, 1)
                act.sem_inc(sims_ready, -1)
                copy(sims[:].rearrange("p g k -> p (g k)"), y.ps[:, 0:2 * HEADS * KEYS], sims_copied)
                yield
                for _ in SELECT[5:-2]:
                    yield
                act.wait_ge(fin_ready, 1)
                act.sem_inc(fin_ready, -1)
                nc.scalar.activation(row_w[:, i, :, :], fin_v[:], ACT.Exp).then_inc(fin_exp, 1)
                yield
                yield

            def gather(b, i):
                act.wait_ge(weights_ready, 1)
                act.sem_inc(weights_ready, -1)
                for g in range(HEADS):
                    use = (HEADS // RING) * i + g // RING + 1
                    act.wait_ge(rows_landed[g % RING], b * (PER_USE * (HEADS // RING) * NT) + PER_USE * use)
                    act.sem_inc(rows_seen, 1)
                    act.wait_ge(rows_seen, 1)
                    act.sem_inc(rows_seen, -1)
                    for r in range(TOPK):
                        row = rows[:, g % RING, r, :]
                        last = nc.scalar.activation(row, row, ACT.Copy, scale=row_w[:, i, g, r:r + 1])
                        if r == TOPK // 2 - 1:
                            yield
                    last.then_inc(rows_scaled, 1)
                    yield
                yield

            def heads(_b, i):
                act.wait_ge(kq_ready, 1)
                act.sem_inc(kq_ready, -1)
                nc.scalar.activation(kT[:, :, i * P:(i + 1) * P],
                                     x.O.rearrange("p (c t) -> p c t", c=4), ACT.Copy)
                copy(vm[:, i, :], kv[:, 1, :, :].rearrange("p g d -> p (g d)"), kv_free)
                copy(qmT[:], x.M, kq_copied, scale=D ** -0.5)
                sets = depth(i + 1)
                yield
                exponential(x, i + 1)
                yield
                for g in range(HEADS):
                    copy_probsT(x, i + 1, g % sets * 2 * BANK, sets)
                    if g + 1 < HEADS:
                        exponential(x, i + 1, g + 1, (g + 1) % sets * 2 * BANK)
                    yield
                act.wait_ge(headsT_ready, 1)
                act.sem_inc(headsT_ready, -1)
                copy(cxT[:], x.M, headsT_copied)
                yield
                yield

            def tail(b, i):
                yield
                copy_xnT(y.xnT[:])
                act.wait_ge(qkv1_ready, 1)
                act.sem_inc(qkv1_ready, -1)
                nc.scalar.activation(q1T[:], y.M[0:D, 0:P], ACT.Identity, bias=bq8[:], scale=D ** -0.5)
                nc.scalar.activation(k1T[:, i * P:(i + 1) * P], y.M[0:D, P:2 * P], ACT.Identity,
                                     bias=bq[:, 1:2]).then_inc(qk1_copied, 1)
                yield
                yield
                exponential(y, i + 1)
                yield
                copy_probsT(y, i + 1)
                yield
                act.wait_ge(ctx1T_ready, 1)
                act.sem_inc(ctx1T_ready, -1)
                copy(ctx1T[:], y.M[0:D, 0:P], ctx1T_copied)
                yield
                yield
                copy_xnT(y.xnT[:])
                yield
                yield
                act.wait_ge(logits_shifted, 1)
                act.sem_inc(logits_shifted, -1)
                nc.scalar.activation(gate[:, 1, :], gate[:, 0, :], ACT.Exp,
                                     accum_out=gate_sum[:, 0:1]).then_inc(gate_exp, 1)
                act.wait_ge(hidden_ready, 1)
                act.sem_inc(hidden_ready, -1)
                for e in range(EXPERTS):
                    last = nc.scalar.activation(gelT[:, e, :], y.ps[:, e * P:(e + 1) * P], ACT.Gelu,
                                                bias=b1_s[:, e:e + 1])
                last.then_inc(gelu_ready, 1)
                yield
                yield
                act.wait_ge(out_ready, 1)
                act.sem_inc(out_ready, -1)
                act.dma_start(out[b, i * P:(i + 1) * P, :], outt[:]).then_inc(out_stored, 16)
                yield

            def loaded():
                act.wait_ge(w_loaded_act, 1)
                act.sem_inc(w_loaded_act, -1)
                nc.scalar.activation(bq8[:], bq[:, 0:1], ACT.Copy, scale=D ** -0.5).then_inc(bq8_ready, 1)
                act.wait_ge(bq8_ready, 1)
                act.sem_inc(bq8_ready, -1)

            all_steps(act, loaded, front, select, gather, heads, tail)
            act.wait_ge(out_stored, 16)

        @block.vector
        def _(dve):
            V = nc.vector

            def step(ins):
                ins.then_inc(dve_step, 1)
                dve.wait_ge(dve_step, 1)
                dve.sem_inc(dve_step, -1)

            def layer_norm(src):
                rs = y.rs
                step(V.bn_stats(y.st6[:], src))
                step(V.bn_aggr(y.mv[:], y.st6[:]))
                step(V.tensor_scalar(rs[:, 0:1], y.mv[:, 1:2], EPS, None, ALU.add))
                V.tensor_scalar(rs[:, 1:2], rs[:, 0:1], 0.5, None, ALU.mult)
                step(V.tensor_scalar(y.rsi[:, 0:1], rs[:, 0:1].bitcast(I32), 1, None, ALU.logical_shift_right))
                step(V.tensor_scalar(rs[:, 2:3].bitcast(I32), y.rsi[:, 0:1], -1.0, RSQRT_SEED, ALU.mult, ALU.add))
                r = 2
                for _ in range(3):
                    step(V.scalar_tensor_tensor(rs[:, 4:5], rs[:, r:r + 1], rs[:, 1:2], rs[:, r:r + 1],
                                                ALU.mult, ALU.mult))
                    step(V.scalar_tensor_tensor(rs[:, 5 - r:6 - r], rs[:, 4:5], 1.5, rs[:, r:r + 1],
                                                ALU.subtract, ALU.mult, reverse0=True))
                    r = 5 - r
                dve.wait_ge(y.xn_free, 1)
                dve.sem_inc(y.xn_free, -1)
                V.tensor_scalar(y.xn[:], src, y.mv[:, 0:1], rs[:, r:r + 1], ALU.subtract, ALU.mult)\
                 .then_inc(y.xn_ready, 1)

            def row_max(t, n, g=0, o=0):
                dve.wait_ge(t.scores_ready, 1)
                dve.sem_inc(t.scores_ready, -1)
                V.tensor_reduce(t.nmax[:, g % 2:g % 2 + 1], t.ps[:, o:o + n * P], AX.X, ALU.max,
                                negate=True).then_inc(t.negmax_ready, 1)

            def row_sum(t, g=0):
                dve.wait_ge(t.ctx_ready, 1)
                dve.sem_inc(t.ctx_ready, -1)
                step(V.reciprocal(t.rinv[:], t.rsum[:, g % 2:g % 2 + 1]))

            def front(b, i):
                hs = h[:, b * NT + i, :]
                yield
                if i < PT_TILES:
                    dve.wait_ge(emb_ready, 1)
                    dve.sem_inc(emb_ready, -1)
                    step(V.tensor_tensor(hs, y.O[:, 0:D], posb[:, i, :], ALU.add))
                    dve.sem_inc(emb_read, 1)
                else:
                    dve.wait_ge(text_loaded, 16 * BATCH)
                    step(V.tensor_copy(hs, text[:, b, :]))
                layer_norm(hs)
                yield
                yield

            def top16(values, spare, best, where, groups):
                for g in groups:
                    last = V.max(best[:, g, 0:8], values[:, g, :])
                step(last)
                for g in groups:
                    V.max_index(where[:, g, 0:8], best[:, g, 0:8], values[:, g, :])
                    last = V.match_replace(spare[:, g, :], best[:, g, 0:8], values[:, g, :], LOWEST)
                step(last)
                for g in groups:
                    last = V.max(best[:, g, 8:16], spare[:, g, :])
                step(last)
                for g in groups:
                    last = V.max_index(where[:, g, 8:16], best[:, g, 8:16], spare[:, g, :])
                step(last)

            def pair_up(dst, first, second):
                for a, na, nb, c in BLOCKS:
                    if na == 1:
                        o, s0, s1 = dst[:, :, c:c + nb], first[:, :, a:a + 1], second[:, :, 0:nb]
                        last = V.tensor_tensor(o, s0.broadcast_to([P, HEADS, nb]), s1, ALU.add)
                    elif nb == 1:
                        o, s0, s1 = dst[:, :, c:c + na], first[:, :, a:a + na], second[:, :, 0:1]
                        last = V.tensor_tensor(o, s0, s1.broadcast_to([P, HEADS, na]), ALU.add)
                    else:
                        o = dst[:, :, c:c + na * nb].rearrange("p g (a b) -> p g a b", b=nb)
                        s0 = first[:, :, a:a + na].unsqueeze(3).broadcast_to([P, HEADS, na, nb])
                        s1 = second[:, :, 0:nb].unsqueeze(2).broadcast_to([P, HEADS, na, nb])
                        last = V.tensor_tensor(o, s0, s1, ALU.add)
                return last

            def select(b, i):
                hs = h[:, b * NT + i, :]
                yield
                row_max(y, NT)
                yield
                yield
                row_sum(y)
                step(V.tensor_scalar(y.rinv[:], y.rinv[:], D ** -0.5, None, ALU.mult))
                step(V.scalar_tensor_tensor(hs, y.M[:, 0:D], y.rinv[:], hs, ALU.mult, ALU.add))
                layer_norm(hs)
                yield
                yield
                dve.wait_ge(sims_copied, 1)
                dve.sem_inc(sims_copied, -1)
                dve.sem_inc(sims_seen, 1)
                for g in range(0, 2 * HEADS, GROUPS):
                    top16(sims, sims2, top_v, top_i, range(g, g + GROUPS))
                    yield
                step(V.tensor_scalar(top_i[:, HEADS:, :], top_i[:, HEADS:, :], float(KEYS), None, ALU.mult))
                pair_up(cand_i[:].rearrange("p c g -> p g c"), top_i[:, 0:HEADS, :], top_i[:, HEADS:, :])
                step(pair_up(cand_v, top_v[:, 0:HEADS, :], top_v[:, HEADS:, :]))
                yield
                for g in range(0, HEADS, GROUPS):
                    top16(cand_v, cand_v2, fin_v, fin_p, range(g, g + GROUPS))
                    yield
                for k in range(HEADS // GROUPS):
                    heads = range(k * GROUPS, (k + 1) * GROUPS)
                    step(V.tensor_copy(fin_t[:], fin_p[:, heads[0]:heads[-1] + 1, :].rearrange("p g r -> p r g")))
                    hot4 = hot[:].rearrange("p c (r g) -> p c r g", g=GROUPS)
                    step(V.tensor_tensor(hot4, fin_t[:].unsqueeze(1).broadcast_to([P, CAND, TOPK, GROUPS]),
                                         places[:].unsqueeze(2).broadcast_to([P, CAND, TOPK, GROUPS]), ALU.is_equal))
                    yield
                    step(V.tensor_tensor(hot4, hot4, cand_i[:, :, heads[0]:heads[-1] + 1].unsqueeze(2)
                                         .broadcast_to([P, CAND, TOPK, GROUPS]), ALU.mult))
                    yield
                    half = CAND // 2
                    step(V.tensor_tensor(hot[:, 0:half, :], hot[:, 0:half, :], hot[:, half:CAND, :], ALU.add))
                    rest = half - half // 2
                    step(V.tensor_tensor(hot[:, rest - half // 2:rest, :], hot[:, rest - half // 2:rest, :],
                                         hot[:, rest:half, :], ALU.add))
                    step(V.tensor_reduce(row_f[:], hot[:, 0:rest, :].rearrange("p c k -> p k c"), AX.X, ALU.add))
                    V.tensor_tensor(row_i[:, i, k, :, :], row_f[:].rearrange("p (r g) -> p r g", g=GROUPS),
                                    head_off[:, heads[0]:heads[-1] + 1].unsqueeze(1).broadcast_to([P, TOPK, GROUPS]),
                                    ALU.add).then_inc(rows_chosen, 1)
                    yield
                step(V.tensor_copy(w_sum[:, 0, :], fin_v[:, :, 0]))
                V.tensor_tensor(fin_v[:], fin_v[:], w_sum[:, 0, :].unsqueeze(2).broadcast_to([P, HEADS, TOPK]),
                                ALU.subtract).then_inc(fin_ready, 1)
                yield
                dve.wait_ge(fin_exp, 1)
                dve.sem_inc(fin_exp, -1)
                step(V.tensor_reduce(w_sum[:, 0, :], row_w[:, i, :, :], AX.X, ALU.add))
                step(V.reciprocal(w_sum[:, 1, :], w_sum[:, 0, :]))
                V.tensor_tensor(row_w[:, i, :, :], row_w[:, i, :, :],
                                w_sum[:, 1, :].unsqueeze(2).broadcast_to([P, HEADS, TOPK]),
                                ALU.mult).then_inc(weights_ready, 1)
                yield

            def gather(b, i):
                yield
                yield
                for g in range(HEADS):
                    if g == 0:
                        dve.wait_ge(kv_free, 1)
                        dve.sem_inc(kv_free, -1)
                    dve.wait_ge(rows_scaled, 1)
                    dve.sem_inc(rows_scaled, -1)
                    slot = rows[:, g % RING, :, :]
                    step(V.tensor_reduce(kv[:, :, g, :], slot.rearrange("p r (w d) -> p w d r", w=2), AX.X, ALU.add))
                    dve.sem_inc(slot_free[g % RING], 1)
                    if g == HEADS - 1:
                        dve.sem_inc(kv_ready, 1)
                    yield
                    if g < HEADS - 1:
                        yield

            def heads(b, i):
                hs = h[:, b * NT + i, :]
                sets = depth(i + 1)

                def outcome(g):
                    row_sum(x, g)
                    V.tensor_scalar(cx[:, g * D:(g + 1) * D], x.M[:, 0:D], x.rinv[:], None, ALU.mult)\
                     .then_inc(x.ctx_read, 1)

                yield
                row_max(x, i + 1)
                yield
                for g in range(HEADS):
                    if sets == 2 and g > 0:
                        outcome(g - 1)
                    if g + 1 < HEADS:
                        row_max(x, i + 1, g + 1, (g + 1) % sets * 2 * BANK)
                    if sets == 1:
                        outcome(g)
                    yield
                if sets == 2:
                    outcome(HEADS - 1)
                yield
                dve.wait_ge(mem_out_ready, 1)
                dve.sem_inc(mem_out_ready, -1)
                step(V.tensor_tensor(hs, x.O[:, 0:D], hs, ALU.add))
                dve.sem_inc(mem_out_read, 1)
                yield

            def tail(b, i):
                hs = h[:, b * NT + i, :]
                layer_norm(hs)
                yield
                yield
                dve.wait_ge(qkv1_ready_dve, 1)
                dve.sem_inc(qkv1_ready_dve, -1)
                V.tensor_tensor(v1[:, i, :], y.O[:, 0:D], bv[:], ALU.add).then_inc(v1_ready, 1)
                yield
                row_max(y, i + 1)
                yield
                yield
                row_sum(y)
                V.tensor_scalar(ctx1[:], y.M[:, 0:D], y.rinv[:], None, ALU.mult).then_inc(y.ctx_read, 1)
                yield
                step(V.tensor_tensor(hs, hs, bproj[:], ALU.add))
                dve.wait_ge(proj_ready, 1)
                dve.sem_inc(proj_ready, -1)
                step(V.tensor_tensor(hs, y.O[:, 0:D], hs, ALU.add))
                layer_norm(hs)
                yield
                yield
                dve.wait_ge(logits_ready, 1)
                dve.sem_inc(logits_ready, -1)
                step(V.tensor_tensor(gate[:, 0, :], y.M[:, 0:EXPERTS], gb[:], ALU.add))
                step(V.tensor_reduce(gate_sum[:, 1:2], gate[:, 0, :], AX.X, ALU.max))
                V.tensor_scalar(gate[:, 0, :], gate[:, 0, :], gate_sum[:, 1:2], None, ALU.subtract)\
                 .then_inc(logits_shifted, 1)
                yield
                yield
                dve.wait_ge(gate_exp, 1)
                dve.sem_inc(gate_exp, -1)
                step(V.reciprocal(gate_sum[:, 1:2], gate_sum[:, 0:1]))
                step(V.tensor_scalar(gate[:, 2, :], gate[:, 1, :], gate_sum[:, 1:2], None, ALU.mult))
                step(V.max(gate[:, 4, :], gate[:, 2, :]))
                step(V.tensor_copy(gate[:, 5, 0:2], gate[:, 4, 0:2]))
                probs16 = gate[:, 2:4, :].rearrange("p a e -> p (a e)")
                rest16 = gate[:, 6:8, :].rearrange("p a e -> p (a e)")
                step(V.match_replace(rest16, gate[:, 5, :], probs16, 0.0))
                step(V.tensor_tensor(gate[:, 4, :], gate[:, 2, :], gate[:, 6, :], ALU.subtract))
                yield
                dve.wait_ge(experts_ready, 1)
                dve.sem_inc(experts_ready, -1)
                step(V.tensor_tensor(ysc[:], y.O.rearrange("p (e d) -> p e d", d=D), b2_s[:], ALU.add))
                dve.sem_inc(experts_read, 1)
                step(V.tensor_tensor(ysc[:], ysc[:], gate[:, 4, :].unsqueeze(2).broadcast_to([P, EXPERTS, D]),
                                     ALU.mult))
                step(V.tensor_reduce(ysum[:], ysc[:].rearrange("p e d -> p d e"), AX.X, ALU.add))
                dve.wait_ge(out_stored, 16)
                dve.sem_inc(out_stored, -16)
                V.tensor_tensor(outt[:], hs, ysum[:], ALU.add).then_inc(out_ready, 1)
                yield

            dve.wait_ge(masks_ready_dve, 1)
            dve.sem_inc(masks_ready_dve, -1)
            step(V.tensor_copy(places[:], cand_v[:, 0, :].unsqueeze(2).broadcast_to([P, CAND, GROUPS])))
            dve.wait_ge(ids_loaded, 16)
            step(V.tensor_copy(ids_f[:, 0, :], ids_s[:]))
            step(V.tensor_scalar(ids_f[:, 1, :], ids_f[:, 0, :], 0.0, float(VOCAB), ALU.is_lt, ALU.mult))
            step(V.tensor_tensor(ids_f[:, 0, :], ids_f[:, 0, :], ids_f[:, 1, :], ALU.add))
            step(V.tensor_scalar(ids_f[:, 0, :], ids_f[:, 0, :], 0.0, float(VOCAB - 1), ALU.max, ALU.min))
            V.tensor_scalar(ids_u[:], ids_f[:, 0, :], float(PLE_GROUPS), float(PLE_LAYER),
                            ALU.mult, ALU.add).then_inc(text_ids_ready, 1)
            step(V.memset(gate[:, 2:8, :], -1.0))
            dve.wait_ge(w_loaded_dve, 1)
            dve.sem_inc(w_loaded_dve, -1)
            step(V.tensor_tensor(posb[:], posb[:], tokb[:].unsqueeze(1).broadcast_to([P, PT_TILES, D]), ALU.add))
            for g in range(RING):
                dve.sem_inc(slot_free[g], 1)
            dve.sem_inc(out_stored, 16)
            for free in (y.xn_free, kv_free):
                dve.sem_inc(free, 1)
            def loaded():
                dve.wait_ge(w_loaded_dve, 1)
                dve.sem_inc(w_loaded_dve, -1)

            all_steps(dve, loaded, front, select, gather, heads, tail)


def kernel(**inputs):
    import numpy as np
    import concourse.bacc as bacc
    from concourse.bass_utils import run_bass_kernel_spmd

    a = {k: np.asarray(v) for k, v in inputs.items()}
    arrays = {
        "x_in": a["x"], "ids": a["x_txt"].T,
        "tok_wT": a["L0_tok_W"].T, "tok_b": a["L0_tok_b"], "pos": a["L0_tok_pos_embed"][0],
        "ple": a["L0_txt_ple_table"].reshape(VOCAB * PLE_GROUPS, D),
        "wqT": a["L0_attn_Wq"].T, "wkT": a["L0_attn_Wk"].T, "wvT": a["L0_attn_Wv"].T,
        "wq_pk": a["L0_ffn_Wq_pk"], "keysT": a["L0_ffn_pk_keys"].transpose(0, 2, 3, 1),
        "wq_mem": a["L0_ffn_Wq"],
        "kv_table": np.concatenate([a["L0_ffn_keys_table"], a["L0_ffn_values_table"]], axis=1),
        "wo": a["L0_ffn_Wo"], "w_qkv": a["L1_attn_W_qkv"], "b_qkv": a["L1_attn_b_qkv"],
        "w_proj": a["L1_attn_W_proj"], "b_proj": a["L1_attn_b_proj"],
        "gate_w": a["L1_ffn_gate_w"], "gate_b": a["L1_ffn_gate_b"],
        "w1": a["L1_ffn_W1"], "b1T": a["L1_ffn_b1"].T, "w2": a["L1_ffn_W2"], "b2": a["L1_ffn_b2"],
    }
    arrays = {k: np.ascontiguousarray(v) for k, v in arrays.items()}
    nc = bacc.Bacc("TRN2", target_bir_lowering=False, num_devices=1)
    args = {k: nc.dram_tensor(k, v.shape, mybir.dt.from_np(v.dtype), kind="ExternalInput").ap()
            for k, v in arrays.items()}
    out = nc.dram_tensor("out", (BATCH, TOKENS, D), F32, kind="ExternalOutput").ap()
    build(nc, out=out, **args)
    result = run_bass_kernel_spmd(nc, [arrays], core_ids=[0])
    return result.results[0]["out"]
```
